# Optimizing a Trainium2 kernel written in Bass

```python
import numpy as np
import jax
import jax.numpy as jnp

def _softmax(x, axis=-1):
    return jax.nn.softmax(x, axis=axis)

def _gelu(x):
    return jax.nn.gelu(x, approximate=True)

def _silu(x):
    return jax.nn.silu(x)

def _sigmoid(x):
    return jax.nn.sigmoid(x)

def _layernorm(x, axis=-1, eps=1e-05):
    m = jnp.mean(x, axis=axis, keepdims=True)
    v = jnp.var(x, axis=axis, keepdims=True)
    return (x - m) / jnp.sqrt(v + eps)

def _scatter_add(tgt, idx, src, axis=0):
    return tgt.at[idx].add(src)

def _segment_sum(src, seg, n):
    return jax.ops.segment_sum(src, seg, n)
kernel_name = 'mk_recurrent_d1_jaxref_r2_9a3359'

def setup_inputs(seed: int=0):
    np.random.seed(seed)
    _w = jnp.asarray

    def _L0_attn_setup():
        import jax, jax.numpy as jnp
        import numpy as np
        D_MODEL = 512
        N_HEADS = 16
        D_K = D_MODEL // N_HEADS
        WINDOW = 256
        NEG_INF = -1e+30
        key = jax.random.key(seed)
        ks = jax.random.split(key, 9)
        d = D_MODEL
        scale = 0.02
        return {'x': jax.random.normal(ks[0], (1, 1024, d), dtype=jnp.float32), 'Wq': jax.random.normal(ks[1], (d, d), dtype=jnp.float32) * scale, 'bq': jax.random.normal(ks[2], (d,), dtype=jnp.float32) * scale, 'Wk': jax.random.normal(ks[3], (d, d), dtype=jnp.float32) * scale, 'bk': jax.random.normal(ks[4], (d,), dtype=jnp.float32) * scale, 'Wv': jax.random.normal(ks[5], (d, d), dtype=jnp.float32) * scale, 'bv': jax.random.normal(ks[6], (d,), dtype=jnp.float32) * scale, 'Wo': jax.random.normal(ks[7], (d, d), dtype=jnp.float32) * scale, 'bo': jax.random.normal(ks[8], (d,), dtype=jnp.float32) * scale}
    _L0_attn_in = _L0_attn_setup()

    def _L0_ffn_setup():
        import jax, jax.numpy as jnp
        import numpy as np
        MAX_VAL = 100.0
        key = jax.random.key(seed)
        k1, k2, k3 = jax.random.split(key, 3)
        B, S, D_IN, D_OUT = (4, 4096, 512, 512)
        x = jax.random.normal(k1, (B, S, D_IN), dtype=jnp.float32)
        weights = jax.random.normal(k2, (D_OUT, D_IN), dtype=jnp.float32)
        scale = jnp.ones((D_OUT,), dtype=jnp.float32)
        bias = jax.random.normal(k3, (D_OUT,), dtype=jnp.float32)
        return {'x': x, 'weights': weights, 'scale': scale, 'bias': bias}
    _L0_ffn_in = _L0_ffn_setup()
    _d = {'L0_attn_x': _L0_attn_in['x'], 'L0_attn_Wq': _L0_attn_in['Wq'], 'L0_attn_bq': _L0_attn_in['bq'], 'L0_attn_Wk': _L0_attn_in['Wk'], 'L0_attn_bk': _L0_attn_in['bk'], 'L0_attn_Wv': _L0_attn_in['Wv'], 'L0_attn_bv': _L0_attn_in['bv'], 'L0_attn_Wo': _L0_attn_in['Wo'], 'L0_attn_bo': _L0_attn_in['bo'], 'L0_ffn_weights': _L0_ffn_in['weights'], 'L0_ffn_scale': _L0_ffn_in['scale'], 'L0_ffn_bias': _L0_ffn_in['bias']}
    _x0 = _d['L0_attn_x']
    _d['L0_attn_x'] = jax.random.normal(jax.random.fold_in(jax.random.key(seed), 1), (8, 1024, 512), dtype=_x0.dtype)
    del _x0
    return _d

def reference(L0_attn_x, L0_attn_Wq, L0_attn_bq, L0_attn_Wk, L0_attn_bk, L0_attn_Wv, L0_attn_bv, L0_attn_Wo, L0_attn_bo, L0_ffn_weights, L0_ffn_scale, L0_ffn_bias):

    def _L0_attn_ref(x, Wq, bq, Wk, bk, Wv, bv, Wo, bo):
        import jax, jax.numpy as jnp
        import numpy as np
        D_MODEL = 512
        N_HEADS = 16
        D_K = D_MODEL // N_HEADS
        WINDOW = 256
        NEG_INF = -1e+30
        B, L, D = x.shape
        H, dk, W = (N_HEADS, D_K, WINDOW)

        def proj(Wm, bm):
            y = jnp.einsum('bld,ed->ble', x, Wm) + bm
            return y.reshape(B, L, H, dk).transpose(0, 2, 1, 3)
        q = proj(Wq, bq)
        k = proj(Wk, bk)
        v = proj(Wv, bv)
        scores = jnp.einsum('bhid,bhjd->bhij', q, k) / jnp.sqrt(jnp.asarray(dk, x.dtype))
        if W < L:
            im = jnp.arange(L) % W
            tile_mask = im[:, None] >= im[None, :]
            scores = jnp.where(tile_mask, scores, NEG_INF)
        probs = jax.nn.softmax(scores, axis=-1)
        attn = jnp.einsum('bhij,bhjd->bhid', probs, v)
        out = attn.transpose(0, 2, 1, 3).reshape(B, L, D)
        out = jnp.einsum('bld,ed->ble', out, Wo) + bo
        return out

    def _L0_ffn_ref(x, weights, scale, bias):
        import jax, jax.numpy as jnp
        import numpy as np
        MAX_VAL = 100.0
        w = (weights >= 0.0).astype(x.dtype) * 2.0 - 1.0
        y = jnp.einsum('bsi,oi->bso', x, w)
        y = y * scale + bias
        y = jnp.clip(y, -MAX_VAL, MAX_VAL)
        return y
    x = L0_attn_x
    xn = _layernorm(x, axis=-1)
    s = _L0_attn_ref(xn, L0_attn_Wq, L0_attn_bq, L0_attn_Wk, L0_attn_bk, L0_attn_Wv, L0_attn_bv, L0_attn_Wo, L0_attn_bo)
    g = _silu(_L0_ffn_ref(xn, L0_ffn_weights, L0_ffn_scale, L0_ffn_bias))
    x = x + s * g
    return x

_drawn_inputs = setup_inputs


def setup_inputs(seed=0):
    import zlib

    import numpy as np

    out = dict(_drawn_inputs(seed))
    spreads = {'L0_ffn_scale': (1.0, 0.2)}
    factors = {'L0_attn_bq': 22.212, 'L0_attn_bk': 64.0, 'L0_ffn_bias': 3.253}
    for name, (base, spread) in spreads.items():
        noise = np.random.default_rng([zlib.crc32(name.encode()), seed]).standard_normal(out[name].shape)
        drawn = base * np.exp(spread * noise) if base else spread * noise
        out[name] = jnp.asarray(drawn.astype(out[name].dtype))
    for name, factor in factors.items():
        out[name] = (out[name] * factor).astype(out[name].dtype)
    return out
```

```python
from contextlib import ExitStack

import numpy as np

import concourse.bass as bass
from concourse import mybir

P = 128
B, L, D = 8, 1024, 512
H, DK = 16, 32
NG = 4
NT = 8
NQS = 2
SW = 32.0
SQ = SW / (DK ** 0.5)
SS = 1.0 / (SW * SW)
EPS = 1e-5
MAXV = 100.0
BIGM = 32768.0

NPT = 12
NSLOT = 6

ALU = mybir.AluOpType
ACT = mybir.ActivationFunctionType
F32 = mybir.dt.float32
F16 = mybir.dt.float16
I32 = mybir.dt.int32
AX = mybir.AxisListType


class Queue:

    def __init__(self):
        self.items = []
        self.seen = {}

    def add(self, fn, waits=(), inc=None):
        need = {}
        for t in waits:
            if t is None:
                continue
            s, v = t
            if self.seen.get(id(s), 0) < v:
                need[id(s)] = (s, max(v, need.get(id(s), (s, 0))[1]))
        for k, (s, v) in need.items():
            self.seen[k] = v
        self.items.append((list(need.values()), fn, inc))

    def run(self, eng):
        for waits, fn, inc in self.items:
            for s, v in waits:
                eng.wait_ge(s, v)
            ins = fn(eng)
            if inc is not None:
                ins.then_inc(inc[0], inc[1])


class Count:

    def __init__(self, sem, step=1):
        self.sem, self.step, self.n = sem, step, 0

    def inc(self):
        self.n += self.step
        return (self.sem, self.step)

    @property
    def token(self):
        return (self.sem, self.n) if self.n else None


def build(nc, x, wqT, wkT, wvT, woT, wfT, bqk_in, bv, bo, fsc, fbi, idf, idh, mq, mk, zrow, out):
    ctx = ExitStack()
    with ctx:
        def sb(name, shape, dt):
            return ctx.enter_context(nc.sbuf_tensor(name, shape, dt))

        def pb(name, shape, dt):
            return ctx.enter_context(nc.psum_tensor(name, shape, dt))

        def cnt(name, step=1):
            return Count(ctx.enter_context(nc.semaphore(name)), step)

        Wh = {k: sb(f"wh_{k}", [P, 4, D], F16) for k in "qkvo"}
        Wl = {k: sb(f"wl_{k}", [P, 4, D], F16) for k in "qkvo"}
        Wf = sb("wf", [P, 4, D], F16)
        xTh = [sb(f"xTh{i}", [P, 4, L], F16) for i in range(2)]
        xTl = [sb(f"xTl{i}", [P, 4, L], F16) for i in range(2)]
        Q4 = [sb(f"Q4_{i}", [P, 4, L], F16) for i in range(2)]
        K4 = [sb(f"K4_{i}", [P, 4, L], F16) for i in range(2)]
        sgh = [sb(f"sgh{i}", [P, L], F16) for i in range(2)]
        sgl = [sb(f"sgl{i}", [P, L], F16) for i in range(2)]
        V = sb("V", [P, NSLOT, NT, P], F32)
        PT = sb("PT", [P, NPT, 512], F32)
        Onh = sb("Onh", [P, NSLOT, L], F16)
        Onl = sb("Onl", [P, NSLOT, L], F16)
        xs = [sb(f"xs{i}", [P, D], F32) for i in range(2)]
        xr = [sb(f"xr{i}", [P, D], F32) for i in range(2)]
        Y = sb("Y", [P, D], F32)
        E = sb("E", [P, D], F32)
        T1 = [sb(f"T1_{i}", [P, D], F32) for i in range(2)]
        Sw = sb("Sw", [P, 4, P], F32)
        Rsb = sb("Rsb", [P, 512], F32)
        Tn = sb("Tn", [P, 512], F32)
        bvb = sb("bvb", [P, D], F32)
        bob = sb("bob", [P, D], F32)
        fsb = sb("fsb", [P, D], F32)
        fbb = sb("fbb", [P, D], F32)
        identf = sb("identf", [P, P], F32)
        identh = sb("identh", [P, P], F16)
        bqk0 = sb("bqk0", [P, 2, NG], F32)
        bqk = sb("bqk", [P, 2, NG], F32)
        st6 = sb("st6", [P, 2, 6], F32)
        mv = sb("mv", [P, 2, 2], F32)
        rs = sb("rs", [P, 2, 3], F32)
        mx = sb("mx", [P, 2, 16], F32)
        a16 = sb("a16", [P, 2, 16], F16)
        sums = sb("sums", [P, 2, 16], F32)
        rsum = sb("rsum", [P, 2, 16], F32)
        cT = sb("cT", [16, 2, P], F16)

        pS = [pb(f"pS{i}", [P, 1024], F32) for i in range(2)]
        pT = [pb(f"pT{i}", [P, 512], F32) for i in range(2)]
        pO = pb("pO", [P, 512], F32)
        pJ = pb("pJ", [P, 512], F32)
        pJc = pJ[0:16, 0:64].bitcast(F16)

        pe, act, dve, pool, sp = Queue(), Queue(), Queue(), Queue(), Queue()
        c_const = cnt("s_const", 16)
        c_w = {k: cnt(f"s_w{k}", 16) for k in "qkvof"}
        c_wh = cnt("s_wh")
        c_wl = cnt("s_wl")
        c_b = cnt("s_b")
        c_x = [cnt(f"s_x{i}", 16) for i in range(2)]
        c_r = [cnt(f"s_r{i}", 16) for i in range(2)]
        c_o = [cnt(f"s_o{i}", 16) for i in range(2)]
        c_ln = cnt("s_ln")
        c_pj = cnt("s_pj")
        c_xh = cnt("s_xh")
        c_xl = cnt("s_xl")
        c_qh = cnt("s_qh")
        c_ql = cnt("s_ql")
        c_qd = [cnt(f"s_qd{i}", 16) for i in range(2)]
        c_sd = [cnt(f"s_sd{i}", 16) for i in range(2)]
        c_v = cnt("s_v")
        c_S = cnt("s_S")
        c_m = cnt("s_m")
        c_a = cnt("s_a")
        c_se = cnt("s_se")
        c_rs = cnt("s_rs")
        c_sw = cnt("s_sw")
        c_ct = cnt("s_ct")
        c_cd = [cnt(f"s_cd{i}", 16) for i in range(2)]
        c_T = cnt("s_T")
        c_p = cnt("s_p")
        c_pv = cnt("s_pv")
        c_R = cnt("s_R")
        c_dv = cnt("s_dv")
        c_oh = cnt("s_oh")
        c_ol = cnt("s_ol")
        c_g = cnt("s_g")
        c_y2 = cnt("s_y2")
        c_e = cnt("s_e")
        c_t1 = cnt("s_t1")
        c_t2 = cnt("s_t2")
        c_f = cnt("s_f")

        pj_free = [None]

        pj_open, pj_later = [False], []

        def when_pj_closed(fn):
            if pj_open[0]:
                pj_later.append(fn)
            else:
                fn()

        def dma(dst, src, waits, c):
            sp.add(lambda e, d=dst, s=src: e.dma_start(d, s), waits, c.inc())

        dma(identf[:, :], idf, [], c_const)
        dma(identh[:, :], idh, [], c_const)
        dma(bqk0[:, :, :], bqk_in, [], c_const)
        for i in range(2):
            for j in range(4):
                dma(Q4[i][96:128, j, :], mq, [], c_const)
                dma(K4[i][96:128, j, :], mk, [], c_const)
        for t, v in ((bvb, bv), (bob, bo), (fsb, fsc), (fbb, fbi)):
            dma(t[:, :], v.rearrange("(a d) -> a d", a=1).broadcast_to([P, D]), [], c_const)

        def stage(i):
            return PT[:, 4 * (i % 2):4 * (i % 2) + 4, :]

        x_view = x.rearrange("b (w t r) d -> b t w r d", w=4, t=NT)
        o_view = out.rearrange("b (w t r) d -> b t w r d", w=4, t=NT)

        ln_slot = {}
        xl_last = [None, None]

        def load_x(b, t):
            i = b * NT + t
            s = i % 2
            for w in range(4):
                dma(xs[s][32 * w:32 * w + 32, :], x_view[b, t, w], [ln_slot.get(i - 2)], c_x[s])

        def ln(b, t):
            i = b * NT + t
            s = i % 2
            dve.add(lambda e: e.bn_stats(st6[:, s, :], xs[s][:, :]), [c_x[s].token, ln_slot.get(i - 2)], c_ln.inc())
            dve.add(lambda e: e.bn_aggr(mv[:, s, :], st6[:, s, :]), [c_ln.token], c_ln.inc())
            v, y, z = (rs[:, s, k:k + 1] for k in range(3))

            def step(fn):
                dve.add(fn, [c_ln.token], c_ln.inc())

            step(lambda e: e.tensor_scalar(v, mv[:, s, 1:2], EPS, None, ALU.add))
            step(lambda e: e.tensor_scalar(z.bitcast(I32), v.bitcast(I32), 1, None, ALU.logical_shift_right))
            step(lambda e: e.tensor_scalar(y.bitcast(I32), z.bitcast(I32), -1.0, 1597463007.0, ALU.mult, ALU.add))
            for _ in range(3):
                step(lambda e: e.tensor_scalar(z, y, y, v, ALU.mult, ALU.mult))
                step(lambda e: e.tensor_scalar(z, z, -0.5, 1.5, ALU.mult, ALU.add))
                step(lambda e: e.tensor_scalar(y, y, z, None, ALU.mult))
            dve.add(lambda e: e.tensor_scalar(xs[s][:, :], xs[s][:, :], mv[:, s, 0:1], y,
                                              ALU.subtract, ALU.mult), [c_ln.token], c_ln.inc())
            return c_ln.token

        ln_token = {}
        fo_done = {}

        def xt_quanta(b, t):
            i = b * NT + t
            s, d = i % 2, b % 2

            def q():
                for c in range(4):
                    waits = [ln_token[i], c_const.token, *pj_free] if c == 0 else []
                    pe.add(lambda e, c=c: e.transpose(pJ[:, c * P:(c + 1) * P], xs[s][:, c * P:(c + 1) * P],
                                                      identf[:, :]), waits, c_pj.inc() if c == 3 else None)
                tok = c_pj.token
                ln_slot[i] = tok
                hi = xTh[d][:, :, t * P:(t + 1) * P]
                lo = xTl[d][:, :, t * P:(t + 1) * P]
                src = pJ[:, :].rearrange("p (c q) -> p c q", c=4)
                act.add(lambda e: e.copy(hi, src), [tok], c_xh.inc())
                dve.add(lambda e: e.tensor_tensor(lo, src, hi, ALU.subtract), [c_xh.token], c_xl.inc())
                pj_free[:] = [c_xh.token, c_xl.token]
                xl_last[d] = (c_xh.token, c_xl.token)
            return [q]

        def mms(out_ap, terms, first, last, waits, count):
            for n, (a, b_) in enumerate(terms):
                pe.add(lambda e, a=a, b_=b_, n=n: e.matmul(out_ap, a, b_, start=first and n == 0,
                                                          stop=last and n == len(terms) - 1),
                       waits if n == 0 else (), count.inc() if last and n == len(terms) - 1 else None)

        def tile_quanta(terms, waits, finish, step=4):
            out_q = []
            for k in range(0, len(terms), step):
                part = terms[k:k + step]

                def q(part=part, first=k == 0, last=k + step >= len(terms)):
                    w = [*waits(), *pj_free] if first else ()
                    pj_open[0] = not last
                    mms(pJ[:, :], part, first, last, w, c_pj)
                    if last:
                        finish(c_pj.token)
                        while pj_later:
                            pj_later.pop(0)()
                out_q.append(q)
            return out_q

        grp_last = {}

        def qk_quanta(gn, which, half):
            b, g = divmod(gn, NG)
            d, key = b % 2, "qk"[which]
            cs = slice(half * 512, half * 512 + 512)
            terms = []
            for c in range(4):
                wh, wl = Wh[key][:, c, g * P:(g + 1) * P], Wl[key][:, c, g * P:(g + 1) * P]
                terms += [(wh, xTh[d][:, c, cs]), (wh, xTl[d][:, c, cs]), (wl, xTh[d][:, c, cs])]
            bias = bqk[:, which, g:g + 1]

            def finish(tok):
                hi, lo = sgh[which][:, cs], sgl[which][:, cs]
                act.add(lambda e: e.activation(hi, pJ[:, :], ACT.Identity, bias=bias),
                        [tok, c_b.token, c_sd[which].token if half == 0 else None], c_qh.inc())
                dve.add(lambda e: e.scalar_tensor_tensor(lo, pJ[:, :], bias, hi, ALU.add, ALU.subtract),
                        [c_qh.token, c_sd[which].token if half == 0 else None], c_ql.inc())
                pj_free[:] = [c_qh.token, c_ql.token]
                if half == 0:
                    return
                u = gn % 2
                dst = (Q4, K4)[which][u]
                w = [c_qh.token, c_ql.token, *grp_last.get(gn - 2, ()), c_const.token]
                parts = (sgh, sgl, sgh) if which == 0 else (sgh, sgh, sgl)
                for r, s in enumerate(parts):
                    for j in range(4):
                        sp.add(lambda e, r=r, s=s, j=j: e.dma_start(dst[32 * r:32 * r + 32, j, :],
                                                                    s[which][32 * j:32 * j + 32, :]),
                               w, c_sd[which].inc())
                if which == 0:
                    sp.add(lambda e: e.dma_start(dst[96:97, :, :], zrow), w, c_sd[which].inc())
                qk_token[gn, which] = c_sd[which].token
            return tile_quanta(terms, lambda: [c_wh.token, c_wl.token, *(xl_last[d])], finish)

        qk_token = {}
        v_token = {}

        def v_quanta(b, t):
            d = b % 2
            ts = slice(t * P, (t + 1) * P)
            terms = []
            for c in range(4):
                terms += [(xTh[d][:, c, ts], Wh["v"][:, c, :]), (xTh[d][:, c, ts], Wl["v"][:, c, :]),
                          (xTl[d][:, c, ts], Wh["v"][:, c, :])]

            def finish(tok):
                g = 0
                while g < NG:
                    s = (NG * b + g) % NSLOT
                    n = min(NG - g, NSLOT - s)
                    cols = slice(g * P, (g + n) * P)
                    dst = V[:, s:s + n, t, :]
                    free = [pv_last.get(NG * b + k - NSLOT) for k in range(g, g + n)]
                    dve.add(lambda e, cols=cols, dst=dst, n=n: e.scalar_tensor_tensor(
                        dst, pJ[:, cols].rearrange("p (n q) -> p n q", n=n), 1.0 / SW,
                        bvb[:, cols].rearrange("p (n q) -> p n q", n=n), ALU.mult, ALU.add),
                        [tok, c_const.token, *free], c_v.inc())
                    g += n
                pj_free[:] = [c_v.token]
                v_token[b] = c_v.token
            return tile_quanta(terms, lambda: [c_wh.token, c_wl.token, *(xl_last[d])], finish)

        store = {}

        def fo_quanta(b, t):
            i = b * NT + t
            s, d = i % 2, b % 2
            ts = slice(t * P, (t + 1) * P)
            ft, ot = [], []
            for c in range(4):
                ft += [(xTh[d][:, c, ts], Wf[:, c, :]), (xTl[d][:, c, ts], Wf[:, c, :])]
            for g in range(NG):
                n = (NG * b + g) % NSLOT
                ot += [(Onh[:, n, ts], Wh["o"][:, g, :]), (Onh[:, n, ts], Wl["o"][:, g, :]),
                       (Onl[:, n, ts], Wh["o"][:, g, :])]

            def finish_f(tok):
                for w in range(4):
                    dma(xr[s][32 * w:32 * w + 32, :], x_view[b, t, w], [store.get(("f", i - 2))], c_r[s])
                last = store.get(("t2", i - 1))
                dve.add(lambda e: e.tensor_tensor(Y[:, :], pJ[:, :], fsb[:, :], ALU.mult),
                        [tok, c_const.token, last], c_g.inc())
                pj_free[:] = [c_g.token]
                pool.add(lambda e: e.tensor_tensor(Y[:, :], Y[:, :], fbb[:, :], ALU.add), [c_g.token], c_y2.inc())
                dve.add(lambda e: e.tensor_scalar(Y[:, :], Y[:, :], MAXV, -MAXV, ALU.min, ALU.max),
                        [c_y2.token], c_g.inc())
                dve.add(lambda e: e.tensor_scalar(E[:, :], Y[:, :], -88.0, None, ALU.max), [c_g.token], c_g.inc())
                act.add(lambda e: e.activation(E[:, :], E[:, :], ACT.Exp, scale=-1.0), [c_g.token], c_e.inc())
                dve.add(lambda e: e.tensor_scalar(E[:, :], E[:, :], 1.0, None, ALU.add), [c_e.token], c_g.inc())
                dve.add(lambda e: e.reciprocal(E[:, :], E[:, :]), [c_g.token], c_g.inc())
                dve.add(lambda e: e.tensor_tensor(E[:, :], Y[:, :], E[:, :], ALU.mult), [c_g.token], c_g.inc())

            def finish_o(tok):
                gate = c_g.token
                dve.add(lambda e: e.scalar_tensor_tensor(T1[s][:, :], pJ[:, :], SS, bob[:, :], ALU.mult, ALU.add),
                        [tok, c_o[s].token], c_t1.inc())
                pj_free[:] = [c_t1.token]
                pool.add(lambda e: e.tensor_tensor(T1[s][:, :], T1[s][:, :], E[:, :], ALU.mult),
                         [c_t1.token, gate], c_t2.inc())
                store["t2", i] = c_t2.token
                pool.add(lambda e: e.tensor_tensor(T1[s][:, :], T1[s][:, :], xr[s][:, :], ALU.add),
                         [c_t2.token, c_r[s].token], c_f.inc())
                store["f", i] = c_f.token
                for w in range(4):
                    dma(o_view[b, t, w], T1[s][32 * w:32 * w + 32, :], [c_f.token], c_o[s])
                fo_done[b] = tok
            return [*tile_quanta(ft, lambda: [c_wh.token, *(xl_last[d])], finish_f),
                    None, *tile_quanta(ot, lambda: [c_ol.token, c_oh.token], finish_o)]

        se_tok, a_tok, sums_free, a16_free, cdma = {}, {}, {}, {}, {}
        S_tiles = [0]
        pend_se = []

        def flush_se():
            while pend_se:
                pend_se.pop(0)()

        def s_tile(n, j, qi):
            gn, qs = divmod(n, NQS)
            u, par = gn % 2, n % 2
            qb = 4 * qs + qi
            i = S_tiles[0]
            S_tiles[0] += 1
            slot = pS[i % 2]
            w = [se_tok.get(i - 2), qk_token[gn, 0], qk_token[gn, 1]]
            qc = slice(qb * P, qb * P + P)
            for k0 in range(0, qb * P, 512):
                k1 = min(k0 + 512, qb * P)
                pe.add(lambda e, k0=k0, k1=k1: e.matmul(slot[:, k0:k1], Q4[u][0:96, j, qc], K4[u][0:96, j, k0:k1],
                                                        start=True, stop=True), w)
                w = ()
            pe.add(lambda e: e.matmul(slot[:, qc], Q4[u][:, j, qc], K4[u][:, j, qc], start=True, stop=True),
                   w, c_S.inc())
            col = 4 * j + qi
            width = (qb + 1) * P
            dve.add(lambda e: e.reduce_max(mx[:, par, col:col + 1], slot[:, 0:width], AX.X), [c_S.token], c_m.inc())
            dve.add(lambda e: e.tensor_scalar(a16[:, par, col:col + 1], mx[:, par, col:col + 1], -SS, None, ALU.mult),
                    [c_m.token, a16_free.get(n - 2)], c_a.inc())
            tok = c_a.token
            flush_se()

            def se():
                act.add(lambda e: e.activation(slot[:, 0:width], slot[:, 0:width], ACT.Exp,
                                               bias=a16[:, par, col:col + 1], scale=SS,
                                               accum_out=sums[:, par, col:col + 1]),
                        [tok, sums_free.get(n - 2)], c_se.inc())
                se_tok[i] = c_se.token
            pend_se.append(se)

        def shift_rows(n):
            gn, qs = divmod(n, NQS)
            u, par = gn % 2, n % 2
            pe.add(lambda e: e.transpose(pJc, a16[:, par, :], identh[:, :]), [c_a.token, c_const.token, *pj_free],
                   c_pj.inc())
            a16_free[n] = c_pj.token
            dve.add(lambda e: e.tensor_copy(cT[:, par, :], pJc), [c_pj.token, cdma.get(n - 2)], c_ct.inc())
            pj_free[:] = [c_ct.token]
            for j in range(4):
                sp.add(lambda e, j=j: e.dma_start(Q4[u][96:97, j, qs * 512:qs * 512 + 512],
                                                  cT[4 * j:4 * j + 4, par, :]), [c_ct.token], c_cd[par].inc())
            cdma[n] = c_cd[par].token

        T_tiles = [0]
        p_tok, pvtok = {}, {}
        pv_last = {}
        o_free = [None]

        def st_tile(n, kb, j):
            gn, qs = divmod(n, NQS)
            u = gn % 2
            i = T_tiles[0]
            T_tiles[0] += 1
            slot = pT[i % 2]
            q0 = max(0, P * (kb - 4 * qs))
            kc = slice(kb * P, kb * P + P)
            w = [p_tok.get(i - 2), cdma[n]]
            if kb >= 4 * qs:
                qa = 512 * qs + q0
                last = q0 + P == 512
                pe.add(lambda e: e.matmul(slot[:, q0:q0 + P], K4[u][:, j, kc], Q4[u][:, j, qa:qa + P],
                                          start=True, stop=True), w, c_T.inc() if last else None)
                w = ()
                q1 = q0 + P
            else:
                q1, last = q0, False
            if not last:
                pe.add(lambda e: e.matmul(slot[:, q1:512], K4[u][0:97, j, kc], Q4[u][0:97, j, 512 * qs + q1:512 * qs + 512],
                                          start=True, stop=True), w, c_T.inc())
            act.add(lambda e: e.activation(PT[:, i % NPT, q0:512], slot[:, q0:512], ACT.Exp, scale=SS),
                    [c_T.token, pvtok.get(i - NPT)], c_p.inc())
            p_tok[i] = c_p.token
            return i

        def pv(n, kb, tiles):
            gn, qs = divmod(n, NQS)
            s = gn % NSLOT
            b = gn // NG
            q0 = max(0, P * (kb - 4 * qs))
            for j, i in enumerate(tiles):
                w = [p_tok[i], v_token[b]] + ([o_free[0]] if kb == 0 else [])
                pe.add(lambda e, j=j, i=i: e.matmul(pO[32 * j:32 * j + 32, q0:512], V[:, s, kb, 32 * j:32 * j + 32],
                                                    PT[:, i % NPT, q0:512], start=kb == 0, stop=kb == 4 * qs + 3),
                       w, c_pv.inc() if j == 3 else None)
            for i in tiles:
                pvtok[i] = c_pv.token

        sw_free = [None]
        rs_free = {}

        def widen_sums(n):
            par = n % 2
            sv = rsum[:, par, :].rearrange("p (j q o) -> p q j o", j=4, o=1)
            dve.add(lambda e: e.reciprocal(rsum[:, par, :], sums[:, par, :]), [c_se.token, rs_free.get(n - 2)],
                    c_rs.inc())
            pool.add(lambda e: e.tensor_copy(Sw[:, :, :].rearrange("p q (j r) -> p q j r", j=4),
                                             sv.broadcast_to([P, 4, 4, 32])), [c_rs.token, sw_free[0]], c_sw.inc())
            sums_free[n] = c_rs.token
            rs_free[n] = c_sw.token

        def sums_rows(n):
            for qi in range(4):
                w = [c_sw.token, c_const.token, *pj_free] if qi == 0 else ()
                pe.add(lambda e, qi=qi: e.transpose(pJ[:, qi * P:(qi + 1) * P], Sw[:, qi, :], identf[:, :]),
                       w, c_pj.inc() if qi == 3 else None)
            sw_free[0] = c_pj.token
            act.add(lambda e: e.activation(Rsb[:, :], pJ[:, :], ACT.Copy, scale=SW), [c_pj.token, c_dv.token],
                    c_R.inc())
            pj_free[:] = [c_R.token]

        def normalise(n):
            gn, qs = divmod(n, NQS)
            s = gn % NSLOT
            cs = slice(qs * 512, qs * 512 + 512)
            b = gn // NG
            dve.add(lambda e: e.tensor_tensor(Tn[:, :], pO[:, :], Rsb[:, :], ALU.mult),
                    [c_pv.token, c_R.token, c_ol.token], c_dv.inc())
            o_free[0] = c_dv.token
            free = [fo_done.get((gn - NSLOT) // NG)] if gn >= NSLOT else []
            pool.add(lambda e: e.tensor_copy(Onh[:, s, cs], Tn[:, :]), [c_dv.token, *free], c_oh.inc())
            pool.add(lambda e: e.tensor_tensor(Onl[:, s, cs], Tn[:, :], Onh[:, s, cs], ALU.subtract),
                     [c_oh.token], c_ol.inc())
            pv_last[gn] = c_pv.token
            grp_last[gn] = (c_S.token if qs == 0 else grp_S[gn], c_T.token)

        grp_S = {}
        NU = B * NG * NQS

        for t in range(2):
            load_x(0, t)
        wsrc = {"q": wqT, "k": wkT, "v": wvT, "o": woT}
        stage_free = [None, None]

        def load_w(i, key):
            dst = stage(i)
            dma(dst, wsrc.get(key, wfT), [stage_free[i % 2]], c_w[key])

        def split_w(i, key):
            src = stage(i)
            if key == "f":
                dve.add(lambda e: e.tensor_scalar(src, src, 0.0, 2.0, ALU.is_ge, ALU.mult), [c_w[key].token], c_wl.inc())
                dve.add(lambda e: e.tensor_scalar(Wf[:, :, :], src, -1.0, None, ALU.add), [c_wl.token], c_wl.inc())
                stage_free[i % 2] = c_wl.token
                return
            sc = SQ if key == "q" else SW
            act.add(lambda e: e.activation(Wh[key][:, :, :], src, ACT.Copy, scale=sc), [c_w[key].token], c_wh.inc())
            dve.add(lambda e: e.scalar_tensor_tensor(Wl[key][:, :, :], src, sc, Wh[key][:, :, :], ALU.mult,
                                                     ALU.subtract), [c_wh.token], c_wl.inc())
            stage_free[i % 2] = c_wl.token

        load_w(0, "q")
        load_w(1, "k")
        dve.add(lambda e: e.tensor_scalar(bqk[:, 0, :], bqk0[:, 0, :], SQ, None, ALU.mult), [c_const.token], c_b.inc())
        dve.add(lambda e: e.tensor_scalar(bqk[:, 1, :], bqk0[:, 1, :], SW, None, ALU.mult), [c_const.token], c_b.inc())

        def run(quanta):
            for q in quanta:
                if q is not None:
                    q()

        for t in range(NT):
            ln_token[t] = ln(0, t)
            run(xt_quanta(0, t))
            if t + 2 < NT:
                load_x(0, t + 2)
            if t == 2:
                split_w(0, "q")
                load_w(2, "v")
            if t == 4:
                split_w(1, "k")
                load_w(3, "f")
        split_w(2, "v")
        load_w(4, "o")
        for half in range(2):
            for which in range(2):
                run(qk_quanta(0, which, half))
        split_w(3, "f")
        split_w(4, "o")
        stage_done = [c_wh.token, c_wl.token]
        for k in range(NPT):
            pvtok[k - NPT] = stage_done[1]

        def filler(n):
            b, r = divmod(n, NG * NQS)
            g, qs = divmod(r, NQS)
            f = []

            def put(quanta):
                f.extend(quanta)
                f.extend([None, None])

            if n < 0:
                for t in range(NT):
                    put(v_quanta(0, t))
                return f
            gn = n // NQS
            if qs == 0 and gn + 1 < B * NG:
                if g == NG - 1 and b + 1 < B:
                    pass
                for half in range(2):
                    for which in range(2):
                        put(qk_quanta(gn + 1, which, half))
            fo = {(0, 1): (0, 1, 2), (1, 0): (3,), (1, 1): (4, 5, 6), (2, 0): (7,)}.get((g, qs), ())
            if b > 0:
                for t in fo:
                    put(fo_quanta(b - 1, t))
            if b + 1 < B:
                if (g, qs) == (2, 1):
                    for t in range(NT):
                        def q(t=t):
                            for x_ in xt_quanta(b + 1, t):
                                x_()
                            if t + 2 < NT:
                                load_x(b + 1, t + 2)
                                ln_token[(b + 1) * NT + t + 2] = ln(b + 1, t + 2)
                        f.extend([q, None, None])
                vt = {(2, 1): (0, 1, 2), (3, 0): (3,), (3, 1): (4, 5, 6, 7)}.get((g, qs), ())
                for t in vt:
                    put(v_quanta(b + 1, t))
            return f

        def period(n):
            main = []
            steps = []
            if n >= 0:
                gn, qs = divmod(n, NQS)
                nkb = 4 * qs + 4
                done = {}

                def st(kb, j):
                    done.setdefault(kb, []).append(st_tile(n, kb, j))
                for kb in range(nkb):
                    for j in range(4):
                        steps.append((4 * kb + j + 0.5, lambda kb=kb, j=j: st(kb, j)))
                    if kb:
                        steps.append((4 * kb + 3.7, lambda kb=kb: pv(n, kb - 1, done[kb - 1])))
                steps.append((4 * nkb + 0.5, lambda: pv(n, nkb - 1, done[nkb - 1])))
                total = 4 * nkb + 1.0
                steps.append((0.2, lambda: widen_sums(n)))
                steps.append((total * 0.5, lambda: when_pj_closed(lambda: sums_rows(n))))
            else:
                total = 16.0
            if n + 1 < NU:
                m = n + 1
                span = total * 0.85
                k = 0
                for qi in range(4):
                    for j in range(4):
                        steps.append(((k + 0.6) / 16 * span, lambda j=j, qi=qi: s_tile(m, j, qi)))
                        k += 1
                steps.append((total * 0.93, lambda: (flush_se(), when_pj_closed(lambda: shift_rows(m)))))
            f = filler(n)
            start = 0.0
            for k, q in enumerate(f):
                if q is not None:
                    steps.append((start + (k + 0.4) / len(f) * (total - start), q))
            steps.sort(key=lambda s: s[0])
            for _, s in steps:
                s()
            if n >= 0:
                normalise(n)
                if n % NQS == 0:
                    pass
            if n + 1 < NU and (n + 1) % NQS == 1:
                grp_S[(n + 1) // NQS] = c_S.token
            b, r = divmod(n, NG * NQS)
            if n >= 0 and r == 4 and b + 1 < B:
                for t in range(2):
                    load_x(b + 1, t)
                    ln_token[(b + 1) * NT + t] = ln(b + 1, t)

        for n in range(-1, NU):
            period(n)
        for t in range(NT):
            run(fo_quanta(B - 1, t))
        for s in range(2):
            sp.add(lambda e: e.nop() if False else None, [c_o[s].token])

        block = ctx.enter_context(nc.Block())

        @block.tensor
        def _(e):
            pe.run(e)

        @block.scalar
        def _(e):
            act.run(e)

        @block.vector
        def _(e):
            dve.run(e)

        @block.gpsimd
        def _(e):
            pool.run(e)

        @block.sync
        def _(e):
            sp.run(e)


def kernel(L0_attn_x, L0_attn_Wq, L0_attn_bq, L0_attn_Wk, L0_attn_bk, L0_attn_Wv, L0_attn_bv, L0_attn_Wo,
           L0_attn_bo, L0_ffn_weights, L0_ffn_scale, L0_ffn_bias):
    import concourse.bacc as bacc
    from concourse.bass_utils import run_bass_kernel_spmd

    def wt(w):
        return np.ascontiguousarray(np.asarray(w).T.reshape(4, P, D).transpose(1, 0, 2))

    r = np.arange(L) % 32
    c = np.arange(31)
    mq = np.zeros((32, L), np.float16)
    mk = np.zeros((32, L), np.float16)
    mq[1:] = np.where(c[:, None] == r[None, :], BIGM, 0.0)
    mk[1:] = np.where(c[:, None] < r[None, :], -BIGM, 0.0)
    mk[0] = SW * SW
    named = {
        "x": np.ascontiguousarray(L0_attn_x),
        "wqT": wt(L0_attn_Wq), "wkT": wt(L0_attn_Wk), "wvT": wt(L0_attn_Wv), "woT": wt(L0_attn_Wo),
        "wfT": wt(L0_ffn_weights),
        "bqk": np.ascontiguousarray(np.stack([np.asarray(v).reshape(NG, P).T for v in (L0_attn_bq, L0_attn_bk)], 1)),
        "bv": np.ascontiguousarray(L0_attn_bv), "bo": np.ascontiguousarray(L0_attn_bo),
        "fsc": np.ascontiguousarray(L0_ffn_scale), "fbi": np.ascontiguousarray(L0_ffn_bias),
        "idf": np.eye(P, dtype=np.float32), "idh": np.eye(P, dtype=np.float16),
        "mq": mq, "mk": mk, "zrow": np.zeros((1, 4, L), np.float16),
    }
    nc = bacc.Bacc("TRN2", target_bir_lowering=False, num_devices=1, dynamic_dma_scratch_size=1024)
    arrays, args = {}, []
    for name, a in named.items():
        arrays[f"in_{name}"] = a
        args.append(nc.dram_tensor(f"in_{name}", a.shape, mybir.dt.from_np(a.dtype), kind="ExternalInput").ap())
    out = nc.dram_tensor("out_0", (B, L, D), F32, kind="ExternalOutput").ap()
    build(nc, *args, out)
    res = run_bass_kernel_spmd(nc, [arrays], core_ids=[0])
    return res.results[0]["out_0"]
```

```python
from contextlib import ExitStack

import numpy as np

import concourse.bass as bass
from concourse import mybir

P = 128
B, L, D = 8, 1024, 512
H, DK = 16, 32
NG = 4
NT = 8
NQS = 2
SW = 32.0
SQ = SW / (DK ** 0.5)
SS = 1.0 / (SW * SW)
EPS = 1e-5
MAXV = 100.0
BIGM = 32768.0

STEP = 4
PLACES = ((0, None), (1, None))
NPT = 8
LATE = 4.0
EASY, HARD = 0.5, 0.0
HOP = 0.12
DMA_HOP = 1.6
FO_DUE, FO_STEP, XT_DUE, QK_DUE, V_DUE = 7.5, 0.4, 2.4, 1.4, 0.7
P_S, P_T, P_PV, P_J, P_LN, P_GATE, P_EVAC = 0.0, 0.0, 0.05, -0.3, 0.4, 0.0, -0.2
NSLOT = 6

ALU = mybir.AluOpType
ACT = mybir.ActivationFunctionType
F32 = mybir.dt.float32
F16 = mybir.dt.float16
I32 = mybir.dt.int32
AX = mybir.AxisListType


class Queue:

    def __init__(self):
        self.items = []
        self.seen = {}

    def add(self, fn, waits=(), inc=None):
        need = {}
        for t in waits:
            if t is None:
                continue
            s, v = t
            if self.seen.get(id(s), 0) < v:
                need[id(s)] = (s, max(v, need.get(id(s), (s, 0))[1]))
        for k, (s, v) in need.items():
            self.seen[k] = v
        self.items.append((list(need.values()), fn, inc))

    def run(self, eng):
        for waits, fn, inc in self.items:
            for s, v in waits:
                eng.wait_ge(s, v)
            ins = fn(eng)
            if inc is not None:
                ins.then_inc(inc[0], inc[1])


class Count:

    def __init__(self, sem, step=1):
        self.sem, self.step, self.n = sem, step, 0

    def inc(self):
        self.n += self.step
        return (self.sem, self.step)

    @property
    def token(self):
        return (self.sem, self.n) if self.n else None


class Bank:

    def __init__(self):
        self.held, self.tokens = False, []

    def give(self, *tokens):
        self.held, self.tokens = False, list(tokens)


class Op:

    def __init__(self, queue, cost, fns, waits, count, prio=0.0, bank=None, each=False):
        self.queue, self.cost, self.fns = queue, cost, fns if isinstance(fns, list) else [fns]
        self.waits, self.count, self.prio, self.bank, self.each = waits, count, prio, bank, each


class Order:

    def __init__(self, dmas):
        self.free, self.ready, self.strands, self.dmas = {}, {}, [], dmas

    def add(self, gen):
        self.step(gen, None)

    def step(self, gen, token):
        try:
            self.strands.append((gen, gen.send(token)))
        except StopIteration:
            pass

    def run(self):
        while self.strands:
            best = None
            for k, (gen, op) in enumerate(self.strands):
                if op.bank is not None and op.bank.held:
                    continue
                try:
                    waits = op.waits() if callable(op.waits) else op.waits
                except KeyError:
                    continue
                if op.bank is not None:
                    waits = [*waits, *op.bank.tokens]
                start = self.free.get(id(op.queue), 0.0)
                for t in waits:
                    if t is not None:
                        start = max(start, self.ready[id(t[0]), t[1]])
                prio = op.prio() if callable(op.prio) else op.prio
                if best is None or start + prio < best[0]:
                    best = (start + prio, start, k, gen, op, waits)
            assert best is not None, "no strand can go on"
            _, start, k, gen, op, waits = best
            del self.strands[k]
            if op.bank is not None:
                op.bank.held = True
            for n, fn in enumerate(op.fns):
                last = n == len(op.fns) - 1
                op.queue.add(fn, waits if n == 0 else (), op.count.inc() if op.count and (last or op.each) else None)
            end = self.free[id(op.queue)] = start + op.cost
            token = None
            if op.count:
                token = op.count.token
                self.ready[id(token[0]), token[1]] = end + (DMA_HOP if op.queue is self.dmas else HOP)
            self.step(gen, token)


def build(nc, x, wqT, wkT, wvT, woT, wfT, bqk_in, bv, bo, fsc, fbi, idf, idh, mq, mk, zrow, out):
    ctx = ExitStack()
    with ctx:
        def sb(name, shape, dt):
            return ctx.enter_context(nc.sbuf_tensor(name, shape, dt))

        def pb(name, shape, dt):
            return ctx.enter_context(nc.psum_tensor(name, shape, dt))

        def cnt(name, step=1):
            return Count(ctx.enter_context(nc.semaphore(name)), step)

        Wh = {k: sb(f"wh_{k}", [P, 4, D], F16) for k in "qkvo"}
        Wl = {k: sb(f"wl_{k}", [P, 4, D], F16) for k in "qkvo"}
        Wf = sb("wf", [P, 4, D], F16)
        xTh = [sb(f"xTh{i}", [P, 4, L], F16) for i in range(2)]
        xTl = [sb(f"xTl{i}", [P, 4, L], F16) for i in range(2)]
        Q4 = [sb(f"Q4_{i}", [P, 4, L], F16) for i in range(2)]
        K4 = [sb(f"K4_{i}", [P, 4, L], F16) for i in range(2)]
        sgh = [sb(f"sgh{i}", [P, L], F16) for i in range(2)]
        sgl = [sb(f"sgl{i}", [P, L], F16) for i in range(2)]
        V = sb("V", [P, NSLOT, NT, P], F32)
        PT = sb("PT", [P, NPT, 512], F32)
        Onh = sb("Onh", [P, NSLOT, L], F16)
        Onl = sb("Onl", [P, NSLOT, L], F16)
        xs = sb("xs", [P, NT, D], F32)
        xr = [sb(f"xr{i}", [P, D], F32) for i in range(2)]
        Y = sb("Y", [P, D], F32)
        E = sb("E", [P, D], F32)
        Z = sb("Z", [P, D], F32)
        U = sb("U", [P, D], F32)
        T1 = sb("T1", [P, D], F32)
        Sw = sb("Sw", [P, 4, P], F32)
        Rsb = sb("Rsb", [P, 512], F32)
        Tn = sb("Tn", [P, 512], F32)
        bvb = sb("bvb", [P, D], F32)
        bob = sb("bob", [P, D], F32)
        fsb = sb("fsb", [P, D], F32)
        fbb = sb("fbb", [P, D], F32)
        identf = sb("identf", [P, P], F32)
        identh = sb("identh", [P, P], F16)
        bqk0 = sb("bqk0", [P, 2, NG], F32)
        bqk = sb("bqk", [P, 2, NG], F32)
        st6 = sb("st6", [P, NT, 6], F32)
        mv = sb("mv", [P, NT, 2], F32)
        rs = sb("rs", [P, 3, NT], F32)
        junk = sb("junk", [P, 2, L], mybir.dt.bfloat16)
        a16 = sb("a16", [P, 2, 16], F16)
        sums = sb("sums", [P, 2, 16], F32)
        rsum = sb("rsum", [P, 2, 16], F32)
        two = sb("two", [P, 1], F32)
        cT = sb("cT", [16, 2, P], F16)

        pS = [pb(f"pS{i}", [P, 1024], F32) for i in range(2)]
        pT = [pb(f"pT{i}", [P, 512], F32) for i in range(2)]
        pO = pb("pO", [P, 512], F32)
        pJ = pb("pJ", [P, 512], F32)
        pJc = pJ[0:16, 0:64].bitcast(F16)

        pe, act, dve, pool, sp = Queue(), Queue(), Queue(), Queue(), Queue()
        c_const = cnt("s_const", 16)
        c_w = {k: cnt(f"s_w{k}", 16) for k in "qkvof"}
        c_wh = cnt("s_wh")
        c_wl = cnt("s_wl")
        c_b = cnt("s_b")
        c_x = [cnt(f"s_x{i}", 16) for i in range(NT)]
        c_r = [cnt(f"s_r{i}", 16) for i in range(2)]
        c_o = [cnt(f"s_o{i}", 16) for i in range(2)]
        c_ln = cnt("s_ln")
        c_pj = cnt("s_pj")
        c_xh = cnt("s_xh")
        c_xl = cnt("s_xl")
        c_qh = cnt("s_qh")
        c_ql = cnt("s_ql")
        c_qd = [cnt(f"s_qd{i}", 16) for i in range(2)]
        c_sd = [cnt(f"s_sd{i}", 16) for i in range(2)]
        c_v = cnt("s_v")
        c_S = cnt("s_S")
        c_a = cnt("s_a")
        c_se = cnt("s_se")
        c_rs = cnt("s_rs")
        c_sw = cnt("s_sw")
        c_ct = cnt("s_ct")
        c_cd = [cnt(f"s_cd{i}", 16) for i in range(2)]
        c_T = cnt("s_T")
        c_p = cnt("s_p")
        c_pv = cnt("s_pv")
        c_R = cnt("s_R")
        c_dv = cnt("s_dv")
        c_oh = cnt("s_oh")
        c_ol = cnt("s_ol")
        c_g = cnt("s_g")
        c_gt = cnt("s_gt")
        c_y2 = cnt("s_y2")
        c_e = cnt("s_e")
        c_t1 = cnt("s_t1")
        c_t2 = cnt("s_t2")
        c_f = cnt("s_f")

        bank = Bank()
        order = Order(sp)
        reached = [0.0]

        def need_by(unit):
            return lambda: HARD if unit - reached[0] < LATE else EASY

        def copy_in(dst, src):
            return lambda e: e.dma_start(dst, src)

        def constants():
            fns = [copy_in(identf[:, :], idf), copy_in(identh[:, :], idh), copy_in(bqk0[:, :, :], bqk_in)]
            for t, v in ((bvb, bv), (bob, bo), (fsb, fsc), (fbb, fbi)):
                fns.append(copy_in(t[:, :], v.rearrange("(a d) -> a d", a=1).broadcast_to([P, D])))
            for i in range(2):
                for j in range(4):
                    fns += [copy_in(Q4[i][96:128, j, :], mq), copy_in(K4[i][96:128, j, :], mk)]
            const["in"] = yield Op(sp, 0.65 * len(fns), fns, [], c_const, each=True)

        const = {}

        def small_constants():
            yield Op(pool, 0.1, lambda e: e.memset(two[:, :], 2.0), [], c_gt)
            yield Op(dve, 0.1, lambda e: e.tensor_scalar(bqk[:, 0, :], bqk0[:, 0, :], SQ, None, ALU.mult),
                     lambda: [const["in"]], c_b)
            const["bias"] = yield Op(dve, 0.1, lambda e: e.tensor_scalar(bqk[:, 1, :], bqk0[:, 1, :], SW, None,
                                                                         ALU.mult), lambda: [const["in"]], c_b)

        wsrc = {"q": wqT, "k": wkT, "v": wvT, "f": wfT, "o": woT}
        w_tok, stage_free = {}, {}

        def load_weights():
            for i, (key, src) in enumerate(wsrc.items()):
                dst = PT[:, 4 * (i % 2):4 * (i % 2) + 4, :]
                w_tok["in", key] = yield Op(sp, 1.0, copy_in(dst, src),
                                            lambda: [stage_free[i - 2]] if i > 1 else [], c_w[key])

        def split_weights():
            for i, key in enumerate(wsrc):
                src = PT[:, 4 * (i % 2):4 * (i % 2) + 4, :]
                loaded = lambda key=key: [w_tok["in", key]]
                if key == "f":
                    t = yield Op(dve, 1.1, lambda e, src=src: e.tensor_scalar(src, src, 0.0, 2.0, ALU.is_ge, ALU.mult),
                                 loaded, c_wl, -0.2)
                    w_tok[key] = stage_free[i] = yield Op(
                        dve, 1.1, lambda e, src=src: e.tensor_scalar(Wf[:, :, :], src, -1.0, None, ALU.add), [t], c_wl, -0.2)
                    continue
                sc = SQ if key == "q" else SW
                for h in range(4):
                    t = yield Op(act, 0.48, lambda e, src=src, key=key, sc=sc, h=h: e.activation(
                        Wh[key][:, h, :], src[:, h, :], ACT.Copy, scale=sc), loaded, c_wh, -0.2)
                    w_tok[key] = yield Op(dve, 0.6, lambda e, src=src, key=key, sc=sc, h=h: e.scalar_tensor_tensor(
                        Wl[key][:, h, :], src[:, h, :], sc, Wh[key][:, h, :], ALU.mult, ALU.subtract), [t], c_wl, -0.2)
                stage_free[i] = w_tok[key]
            for k in range(NPT):
                pvtok[k - NPT] = w_tok["o"]

        x_view = x.rearrange("b (w t r) d -> b t w r d", w=4, t=NT)
        o_view = out.rearrange("b (w t r) d -> b t w r d", w=4, t=NT)
        x_tok, xs_free, ln_tok, xt_tok, ff_tok, fo_tok = {}, {}, {}, {}, {}, {}

        def load_x():
            for b in range(B):
                for t in range(NT):
                    for w in range(4):
                        x_tok[b, t] = yield Op(sp, 0.65, copy_in(xs[32 * w:32 * w + 32, t, :], x_view[b, t, w]),
                                               lambda: [xs_free[b - 1, t]] if b else [], c_x[t],
                                               -1.0 if b == 0 else P_LN)
                    if w == 3:
                        loaded[b, t] = x_tok[b, t]

        loaded = {}

        def layer_norm():
            v, y, z = (rs[:, k, :] for k in range(3))
            for b in range(B):
                last = None
                prio = -0.1 if b == 0 else P_LN
                for t in range(NT):
                    st = yield Op(dve, 0.6, lambda e, t=t: e.bn_stats(st6[:, t, :], xs[:, t, :]),
                                  lambda: [loaded[b, t], last], c_ln, prio)
                    last = yield Op(dve, 0.1, lambda e, t=t: e.bn_aggr(mv[:, t, :], st6[:, t, :]), [st], c_ln, prio)
                ops = [lambda e: e.tensor_scalar(v, mv[:, :, 1], EPS, None, ALU.add),
                       lambda e: e.tensor_scalar(z.bitcast(I32), v.bitcast(I32), 1, None, ALU.logical_shift_right),
                       lambda e: e.tensor_scalar(y.bitcast(I32), z.bitcast(I32), -1.0, 1597463007.0, ALU.mult,
                                                 ALU.add)]
                for _ in range(3):
                    ops += [lambda e: e.tensor_tensor(z, y, y, ALU.mult),
                            lambda e: e.tensor_tensor(z, z, v, ALU.mult),
                            lambda e: e.tensor_scalar(z, z, -0.5, 1.5, ALU.mult, ALU.add),
                            lambda e: e.tensor_tensor(y, y, z, ALU.mult)]
                for f in ops:
                    last = yield Op(dve, 0.07, f, [last], c_ln, prio)
                for t in range(NT):
                    ln_tok[b, t] = yield Op(dve, 0.35, lambda e, t=t: e.tensor_scalar(
                        xs[:, t, :], xs[:, t, :], mv[:, t, 0:1], rs[:, 1, t:t + 1], ALU.subtract, ALU.mult),
                        [last], c_ln, prio)
                last = ln_tok[b, NT - 1]

        def transpose_x(b):
            d = b % 2
            for t in range(NT):
                fns = [lambda e, t=t, c=c: e.transpose(pJ[:, c * P:(c + 1) * P], xs[:, t, c * P:(c + 1) * P],
                                                       identf[:, :]) for c in range(4)]
                tok = yield Op(pe, 0.44, fns, lambda: [ln_tok[b, t], const["in"], ff_tok[b - 2, t] if b > 1
                                                       else None], c_pj, need_by(8 * b - XT_DUE + 0.1 * t), bank)
                xs_free[b, t] = tok
                hi = xTh[d][:, :, t * P:(t + 1) * P]
                lo = xTl[d][:, :, t * P:(t + 1) * P]
                src = pJ[:, :].rearrange("p (c q) -> p c q", c=4)
                high = yield Op(dve, 0.6, lambda e, hi=hi: e.tensor_copy(hi, src), [tok], c_xh, P_EVAC)
                low = yield Op(dve, 0.6, lambda e, hi=hi, lo=lo: e.tensor_tensor(lo, src, hi, ALU.subtract),
                               [high], c_xl, P_EVAC)
                bank.give(high, low)
                xt_tok[b, t] = (high, low)

        def product(terms, waits, prio):
            tok = None
            for k in range(0, len(terms), STEP):
                fns = [lambda e, a=a, b_=b_, n=k + n: e.matmul(pJ[:, :], a, b_, start=n == 0,
                                                               stop=n == len(terms) - 1)
                       for n, (a, b_) in enumerate(terms[k:k + STEP])]
                last = k + STEP >= len(terms)
                tok = yield Op(pe, 0.216 * len(fns), fns, waits if k == 0 else [], c_pj if last else None, prio,
                               bank if k == 0 else None)
            return tok

        staged, qk_tok, grp_S, grp_T = {}, {}, {}, {}

        def project_qk():
            for gn in range(B * NG):
                b, g = divmod(gn, NG)
                d = b % 2
                for which, half in ((0, 0), (1, 0), (0, 1), (1, 1)):
                    key = "qk"[which]
                    cs = slice(half * 512, half * 512 + 512)
                    terms = []
                    for c in range(4):
                        wh, wl = Wh[key][:, c, g * P:(g + 1) * P], Wl[key][:, c, g * P:(g + 1) * P]
                        terms += [(wh, xTh[d][:, c, cs]), (wl, xTh[d][:, c, cs]), (wh, xTl[d][:, c, cs])]

                    def waits(key=key, which=which, half=half, gn=gn, b=b):
                        placed = [qk_tok[gn - 1, which, half]] if gn else []
                        return [w_tok[key], const["bias"], *xt_tok[b, 4 * half + 3], *placed]
                    tok = yield from product(terms, waits, need_by(2 * gn - QK_DUE + 0.1 * (2 * half + which)))
                    order.add(stage_qk(gn, which, half, tok))

        def stage_qk(gn, which, half, tok):
            cs = slice(half * 512, half * 512 + 512)
            bias = bqk[:, which, gn % NG:gn % NG + 1]
            hi, lo = sgh[which][:, cs], sgl[which][:, cs]
            placed = qk_tok[gn - 1, which, half] if gn else None
            high = yield Op(act, 0.57, lambda e: e.activation(hi, pJ[:, :], ACT.Identity, bias=bias),
                            [tok, const["bias"], placed], c_qh, P_EVAC)
            low = yield Op(dve, 0.6, lambda e: e.scalar_tensor_tensor(lo, pJ[:, :], bias, hi, ALU.add, ALU.subtract),
                           [high, placed], c_ql, P_EVAC)
            bank.give(high, low)
            staged[gn, which, half] = (high, low)

        def place_qk():
            for gn in range(B * NG):
                for which, half in PLACES:
                    dst = (Q4, K4)[which][gn % 2]
                    halves = (half,) if half is not None else (0, 1)
                    cs = slice(512 * halves[0], 512 * halves[-1] + 512)

                    def waits(gn=gn, which=which, halves=halves):
                        free = [grp_S[gn - 2], grp_T[gn - 2]] if gn > 1 else []
                        return [t for h in halves for t in staged[gn, which, h]] + [const["in"]] + free
                    parts = (sgh, sgl, sgh) if which == 0 else (sgh, sgh, sgl)
                    for r, s in enumerate(parts):
                        for j in range(4):
                            tok = yield Op(sp, 0.65, copy_in(dst[32 * r:32 * r + 32, j, cs],
                                                             s[which][32 * j:32 * j + 32, cs]), waits, c_sd[which], 0.1)
                    if which == 0:
                        tok = yield Op(sp, 0.65, copy_in(dst[96:97, :, cs], zrow[:, :, cs]), waits, c_sd[which], 0.1)
                    for h in halves:
                        qk_tok[gn, which, h] = tok

        v_tok, pv_last = {}, {}

        def project_v(b):
            d = b % 2
            for t in range(NT):
                ts = slice(t * P, (t + 1) * P)
                terms = []
                for c in range(4):
                    terms += [(xTh[d][:, c, ts], Wh["v"][:, c, :]), (xTh[d][:, c, ts], Wl["v"][:, c, :]),
                              (xTl[d][:, c, ts], Wh["v"][:, c, :])]

                def waits(t=t):
                    for g in range(NG):
                        if NG * b + g >= NSLOT:
                            pv_last[NG * b + g - NSLOT]
                    return [w_tok["v"], *xt_tok[b, t]]
                tok = yield from product(terms, waits, need_by(8 * b - V_DUE + 0.3 * t / 8))
                order.add(store_v(b, t, tok))

        def store_v(b, t, tok):
            g = 0
            while g < NG:
                s = (NG * b + g) % NSLOT
                n = min(NG - g, NSLOT - s)
                cols = slice(g * P, (g + n) * P)
                dst = V[:, s:s + n, t, :]
                free = [pv_last[NG * b + k - NSLOT] for k in range(g, g + n) if NG * b + k >= NSLOT]
                tok_v = yield Op(dve, 0.07 + 0.133 * n, lambda e, cols=cols, dst=dst, n=n: e.scalar_tensor_tensor(
                    dst, pJ[:, cols].rearrange("p (n q) -> p n q", n=n), 1.0 / SW,
                    bvb[:, cols].rearrange("p (n q) -> p n q", n=n), ALU.mult, ALU.add),
                    [tok, const["in"], *free], c_v, P_EVAC)
                g += n
            bank.give(tok_v)
            v_tok[b, t] = tok_v

        xr_tok, gate_tok, t2_tok, f_tok = {}, {}, {}, {}

        def gate_and_output(b):
            d = b % 2
            for t in range(NT):
                i = b * NT + t
                ts = slice(t * P, (t + 1) * P)
                ft, ot = [], []
                for c in range(4):
                    ft += [(xTh[d][:, c, ts], Wf[:, c, :]), (xTl[d][:, c, ts], Wf[:, c, :])]
                for g in range(NG):
                    n = (NG * b + g) % NSLOT
                    ot += [(Onh[:, n, ts], Wh["o"][:, g, :]), (Onh[:, n, ts], Wl["o"][:, g, :]),
                           (Onl[:, n, ts], Wh["o"][:, g, :])]
                unit = 8 * b + 6 + t // 4
                due = need_by(8 * b + FO_DUE + FO_STEP * t)
                tok = yield from product(ft, lambda: [w_tok["f"], *xt_tok[b, t], gate_tok[i - 1] if i else None], due)
                ff_tok[b, t] = tok
                order.add(gate(i, b, t, tok))
                tok = yield from product(ot, lambda: [w_tok["o"], oh_tok[unit], ol_tok[unit], gate_tok[i]], due)
                fo_tok[b, t] = tok
                order.add(result(i, b, t, tok))

        def gate(i, b, t, tok):
            s = i % 2
            order.add(reload_x(i, b, t))
            last = gate_tok[i - 1] if i else None
            y1 = yield Op(dve, 0.6, lambda e: e.tensor_tensor(Y[:, :], pJ[:, :], fsb[:, :], ALU.mult),
                          [tok, const["in"], last], c_g, P_EVAC)
            bank.give(y1)
            y2 = yield Op(pool, 1.11, lambda e: e.tensor_tensor(Y[:, :], Y[:, :], fbb[:, :], ALU.add), [y1], c_y2)
            e1 = yield Op(dve, 0.34, lambda e: e.tensor_scalar(E[:, :], Y[:, :], MAXV, -87.0, ALU.min, ALU.max),
                          [y2], c_g, P_GATE)
            y3 = yield Op(dve, 0.34, lambda e: e.tensor_scalar(Y[:, :], Y[:, :], MAXV, -MAXV, ALU.min, ALU.max),
                          [y2], c_g, P_GATE)
            e2 = yield Op(act, 0.48, lambda e: e.activation(E[:, :], E[:, :], ACT.Exp, scale=-1.0), [e1], c_e, P_GATE)
            e3 = yield Op(dve, 0.34, lambda e: e.tensor_scalar(E[:, :], E[:, :], 1.0, None, ALU.add), [e2], c_g, P_GATE)
            z = yield Op(dve, 0.34, lambda e: e.tensor_scalar(Z[:, :].bitcast(I32), E[:, :].bitcast(I32), -1.0,
                                                              2129859011.0, ALU.mult, ALU.add), [e3], c_g, P_GATE)
            for k in range(3):
                u = yield Op(pool, 1.11, lambda e: e.tensor_tensor(U[:, :], E[:, :], Z[:, :], ALU.mult),
                             lambda: [z, t2_tok[i - 1] if i else None], c_gt)
                z = yield Op(dve, 0.6, lambda e, k=k: e.scalar_tensor_tensor(
                    Z[:, :], U[:, :], 2.0 if k else -2.0, Z[:, :], ALU.add, ALU.mult), [u], c_g, P_GATE)
            gate_tok[i] = yield Op(pool, 1.11, lambda e: e.tensor_tensor(U[:, :], Y[:, :], Z[:, :], ALU.mult),
                                   [z, y3], c_gt)

        def reload_x(i, b, t):
            s = i % 2
            stored = c_o[s].token
            for w in range(4):
                xr_tok[i] = yield Op(sp, 0.65, copy_in(xr[s][32 * w:32 * w + 32, :], x_view[b, t, w]), [stored],
                                     c_r[s], 0.2)
            xr_full[i] = xr_tok[i]

        xr_full = {}

        def result(i, b, t, tok):
            s = i % 2
            t1 = yield Op(dve, 0.6, lambda e: e.scalar_tensor_tensor(T1[:, :], pJ[:, :], -SS, bob[:, :], ALU.mult,
                                                                     ALU.subtract),
                          [tok, const["in"], f_tok.get(i - 1)], c_t1, P_EVAC)
            bank.give(t1)
            t2 = t2_tok[i] = yield Op(pool, 1.11, lambda e: e.tensor_tensor(T1[:, :], T1[:, :], U[:, :], ALU.mult),
                                      [t1, gate_tok[i]], c_t2)
            f = f_tok[i] = yield Op(pool, 1.11, lambda e: e.tensor_tensor(xr[s][:, :], T1[:, :], xr[s][:, :], ALU.add),
                                    lambda: [t2, xr_full[i]], c_f)
            for w in range(4):
                yield Op(sp, 0.65, copy_in(o_view[b, t, w], xr[s][32 * w:32 * w + 32, :]), [f], c_o[s], 0.2)

        NU = B * NG * NQS
        s_tiles = [(m, qi, j) for m in range(NU) for qi in range(4) for j in range(4)]
        S_tok, se_tok, a_tok, a_last, se_last = {}, {}, {}, {}, {}
        a16_free, sums_free, cdma = {}, {}, {}

        def scores():
            for i, (m, qi, j) in enumerate(s_tiles):
                gn, qs = divmod(m, NQS)
                u, qb, slot = gn % 2, 4 * qs + qi, pS[i % 2]
                qc = slice(qb * P, qb * P + P)
                fns, cost = [], 0.056
                for k0 in range(0, qb * P, 512):
                    k1 = min(k0 + 512, qb * P)
                    cost += (k1 - k0) * 0.216 / 512
                    fns.append(lambda e, k0=k0, k1=k1, slot=slot, u=u, j=j, qc=qc: e.matmul(
                        slot[:, k0:k1], Q4[u][0:96, j, qc], K4[u][0:96, j, k0:k1], start=True, stop=True))
                fns.append(lambda e, slot=slot, u=u, j=j, qc=qc: e.matmul(
                    slot[:, qc], Q4[u][:, j, qc], K4[u][:, j, qc], start=True, stop=True))

                def waits():
                    placed = [qk_tok[gn, w, h] for w in range(2) for h in range(qs + 1)]
                    return [se_tok[i - 2] if i > 1 else None, *placed]
                S_tok[i] = yield Op(pe, cost, fns, waits, c_S, P_S)
                grp_S[gn] = S_tok[i] if (qs, qi, j) == (1, 3, 3) else None
                if grp_S[gn] is None:
                    del grp_S[gn]

        def shifts():
            for i, (m, qi, j) in enumerate(s_tiles):
                par, col, width = m % 2, 4 * j + qi, (4 * (m % NQS) + qi + 1) * P
                a_tok[i] = yield Op(dve, 0.1 + 0.00104 * width, lambda e, i=i, width=width, par=par, col=col:
                                    e.tensor_scalar(junk[:, i % 2, 0:width], pS[i % 2][:, 0:width], -SS, 3e38,
                                                    ALU.mult, ALU.min, accum_out=a16[:, par, col:col + 1]),
                                    lambda: [S_tok[i], a16_free[m - 2] if m > 1 else None, a_tok.get(i - 2)], c_a)
                if (qi, j) == (3, 3):
                    a_last[m] = a_tok[i]

        def row_sums():
            for i, (m, qi, j) in enumerate(s_tiles):
                par, col, width = m % 2, 4 * j + qi, (4 * (m % NQS) + qi + 1) * P
                se_tok[i] = yield Op(act, 0.24 + 0.000833 * width, lambda e, i=i, width=width, par=par, col=col:
                                     e.activation(pS[i % 2][:, 0:width], pS[i % 2][:, 0:width], ACT.Exp,
                                                  bias=a16[:, par, col:col + 1], scale=SS,
                                                  accum_out=sums[:, par, col:col + 1]),
                                     lambda: [a_tok[i], sums_free[m - 2] if m > 1 else None], c_se)
                if (qi, j) == (3, 3):
                    se_last[m] = se_tok[i]

        def shift_rows():
            for m in range(NU):
                gn, qs = divmod(m, NQS)
                u, par = gn % 2, m % 2
                tok = yield Op(pe, 0.06, lambda e, par=par: e.transpose(pJc, a16[:, par, :], identh[:, :]),
                               lambda: [a_last[m], const["in"], cdma[m - 2] if m > 1 else None], c_pj, P_J, bank)
                a16_free[m] = tok
                ct = yield Op(dve, 0.13, lambda e, par=par: e.tensor_copy(cT[:, par, :], pJc),
                              [tok, cdma.get(m - 2)], c_ct, P_EVAC)
                bank.give(ct)
                fns = [copy_in(Q4[u][96:97, j, qs * 512:qs * 512 + 512], cT[4 * j:4 * j + 4, par, :])
                       for j in range(4)]
                cdma[m] = yield Op(sp, 2.6, fns, [ct], c_cd[par], -2.0, each=True)

        t_tiles = [(n, kb, j) for n in range(NU) for kb in range(4 * (n % NQS) + 4) for j in range(4)]
        T_tok, p_tok, pvtok, pv_tok, o_free = {}, {}, {}, {}, {}

        def scores_t():
            for i, (n, kb, j) in enumerate(t_tiles):
                gn, qs = divmod(n, NQS)
                u, slot = gn % 2, pT[i % 2]
                q0 = max(0, P * (kb - 4 * qs))
                kc = slice(kb * P, kb * P + P)
                fns, cost, q1 = [], 0.0, q0
                if kb >= 4 * qs:
                    qa, q1 = 512 * qs + q0, q0 + P
                    cost += 0.056
                    fns.append(lambda e, slot=slot, u=u, j=j, kc=kc, q0=q0, qa=qa: e.matmul(
                        slot[:, q0:q0 + P], K4[u][:, j, kc], Q4[u][:, j, qa:qa + P], start=True, stop=True))
                if q1 < 512:
                    cost += (512 - q1) * 0.216 / 512
                    fns.append(lambda e, slot=slot, u=u, j=j, kc=kc, q1=q1, qs=qs: e.matmul(
                        slot[:, q1:512], K4[u][0:97, j, kc], Q4[u][0:97, j, 512 * qs + q1:512 * qs + 512],
                        start=True, stop=True))
                T_tok[i] = yield Op(pe, cost, fns, lambda: [p_tok[i - 2] if i > 1 else None, cdma[n]], c_T, P_T)
                if (qs, kb, j) == (1, 7, 3):
                    grp_T[gn] = T_tok[i]

        def probabilities():
            for i, (n, kb, j) in enumerate(t_tiles):
                q0 = max(0, P * (kb - 4 * (n % NQS)))
                p_tok[i] = yield Op(act, 0.06 + 0.000833 * (512 - q0), lambda e, i=i, q0=q0: e.activation(
                    PT[:, i % NPT, q0:512], pT[i % 2][:, q0:512], ACT.Exp, scale=SS),
                    lambda: [T_tok[i], pvtok[i - NPT]], c_p)

        def outputs():
            i = 0
            for n in range(NU):
                gn, qs = divmod(n, NQS)
                s, b, nkb = gn % NSLOT, gn // NG, 4 * qs + 4
                for kb in range(nkb):
                    q0 = max(0, P * (kb - 4 * qs))
                    for j in range(4):
                        fn = (lambda e, j=j, i=i, s=s, kb=kb, q0=q0, last=kb == nkb - 1: e.matmul(
                            pO[32 * j:32 * j + 32, q0:512], V[:, s, kb, 32 * j:32 * j + 32],
                            PT[:, i % NPT, q0:512], start=kb == 0, stop=last))

                        def waits(i=i, n=n, b=b, kb=kb):
                            return [p_tok[i], v_tok[b, kb], o_free[n - 1] if n and kb == 0 else None]
                        pvtok[i] = yield Op(pe, (512 - q0) * 0.234 / 512, fn, waits, c_pv, P_PV)
                        i += 1
                    reached[0] = n + (kb + 1) / nkb
                pv_tok[n] = pvtok[i - 1]
                if qs == 1:
                    pv_last[gn] = pv_tok[n]

        rs_free, sw_free, R_tok, dv_tok, oh_tok, ol_tok = {}, {}, {}, {}, {}, {}

        def inverse_sums():
            for n in range(NU):
                par = n % 2
                sv = rsum[:, par, :].rearrange("p (j q o) -> p q j o", j=4, o=1)
                r = yield Op(dve, 0.17, lambda e, par=par: e.reciprocal(rsum[:, par, :], sums[:, par, :]),
                             lambda: [se_last[n], rs_free.get(n - 2)], c_rs, 0.2)
                sw = yield Op(dve, 0.6, lambda e, sv=sv: e.tensor_copy(
                    Sw[:, :, :].rearrange("p q (j r) -> p q j r", j=4), sv.broadcast_to([P, 4, 4, 32])),
                    lambda: [r, sw_free.get(n - 1)], c_sw, 0.2)
                sums_free[n], rs_free[n] = r, sw
                fns = [lambda e, qi=qi: e.transpose(pJ[:, qi * P:(qi + 1) * P], Sw[:, qi, :], identf[:, :])
                       for qi in range(4)]
                tok = yield Op(pe, 0.44, fns, lambda: [sw, const["in"], dv_tok[n - 1] if n else None], c_pj,
                               P_J, bank)
                sw_free[n] = tok
                R_tok[n] = yield Op(dve, 0.6, lambda e: e.tensor_scalar(Rsb[:, :], pJ[:, :], SW, None, ALU.mult),
                                    [tok, dv_tok.get(n - 1)], c_R, P_EVAC)
                bank.give(R_tok[n])

        def normalise():
            for n in range(NU):
                gn, qs = divmod(n, NQS)
                s = gn % NSLOT
                cs = slice(qs * 512, qs * 512 + 512)
                dv = yield Op(dve, 0.6, lambda e: e.tensor_tensor(Tn[:, :], pO[:, :], Rsb[:, :], ALU.mult),
                              lambda: [pv_tok[n], R_tok[n], ol_tok.get(n - 1)], c_dv, -0.3)
                o_free[n] = dv_tok[n] = dv
                oh_tok[n] = yield Op(dve, 0.34, lambda e, s=s, cs=cs: e.tensor_copy(Onh[:, s, cs], Tn[:, :]),
                                     lambda: [dv, fo_tok[(gn - NSLOT) // NG, 4 * qs + 3] if gn >= NSLOT else None],
                                     c_oh, 0.1)
                ol_tok[n] = yield Op(pool, 1.11, lambda e, s=s, cs=cs: e.tensor_tensor(
                    Onl[:, s, cs], Tn[:, :], Onh[:, s, cs], ALU.subtract), [oh_tok[n]], c_ol, -0.3)

        def chained(make):
            for b in range(B):
                yield from make(b)

        for strand in (load_x(), load_weights(), constants(), small_constants(), layer_norm(), split_weights(),
                       chained(transpose_x), project_qk(), place_qk(), chained(project_v), chained(gate_and_output),
                       scores(), shifts(), row_sums(), shift_rows(), scores_t(), probabilities(), outputs(),
                       inverse_sums(), normalise()):
            order.add(strand)
        order.run()

        block = ctx.enter_context(nc.Block())

        @block.tensor
        def _(e):
            pe.run(e)

        @block.scalar
        def _(e):
            act.run(e)

        @block.vector
        def _(e):
            dve.run(e)

        @block.gpsimd
        def _(e):
            pool.run(e)

        @block.sync
        def _(e):
            sp.run(e)
            for c in c_o:
                e.wait_ge(*c.token)


def kernel(L0_attn_x, L0_attn_Wq, L0_attn_bq, L0_attn_Wk, L0_attn_bk, L0_attn_Wv, L0_attn_bv, L0_attn_Wo,
           L0_attn_bo, L0_ffn_weights, L0_ffn_scale, L0_ffn_bias):
    import concourse.bacc as bacc
    from concourse.bass_utils import run_bass_kernel_spmd

    def wt(w):
        return np.ascontiguousarray(np.asarray(w).T.reshape(4, P, D).transpose(1, 0, 2))

    r = np.arange(L) % 32
    c = np.arange(31)
    mq = np.zeros((32, L), np.float16)
    mk = np.zeros((32, L), np.float16)
    mq[1:] = np.where(c[:, None] == r[None, :], BIGM, 0.0)
    mk[1:] = np.where(c[:, None] < r[None, :], -BIGM, 0.0)
    mk[0] = SW * SW
    named = {
        "x": np.ascontiguousarray(L0_attn_x),
        "wqT": wt(L0_attn_Wq), "wkT": wt(L0_attn_Wk), "wvT": wt(L0_attn_Wv), "woT": wt(L0_attn_Wo),
        "wfT": wt(L0_ffn_weights),
        "bqk": np.ascontiguousarray(np.stack([np.asarray(v).reshape(NG, P).T for v in (L0_attn_bq, L0_attn_bk)], 1)),
        "bv": np.ascontiguousarray(L0_attn_bv), "bo": np.ascontiguousarray(L0_attn_bo),
        "fsc": np.ascontiguousarray(L0_ffn_scale), "fbi": np.ascontiguousarray(L0_ffn_bias),
        "idf": np.eye(P, dtype=np.float32), "idh": np.eye(P, dtype=np.float16),
        "mq": mq, "mk": mk, "zrow": np.zeros((1, 4, L), np.float16),
    }
    nc = bacc.Bacc("TRN2", target_bir_lowering=False, num_devices=1, dynamic_dma_scratch_size=1024)
    arrays, args = {}, []
    for name, a in named.items():
        arrays[f"in_{name}"] = a
        args.append(nc.dram_tensor(f"in_{name}", a.shape, mybir.dt.from_np(a.dtype), kind="ExternalInput").ap())
    out = nc.dram_tensor("out_0", (B, L, D), F32, kind="ExternalOutput").ap()
    build(nc, *args, out)
    res = run_bass_kernel_spmd(nc, [arrays], core_ids=[0])
    return res.results[0]["out_0"]
```

```python
from contextlib import ExitStack

import numpy as np

import concourse.bass as bass
from concourse import mybir

P = 128
B, L, D = 8, 1024, 512
H, DK = 16, 32
NG = 4
NT = 8
NQS = 2
SW = 32.0
SQ = SW / (DK ** 0.5)
SS = 1.0 / (SW * SW)
EPS = 1e-5
MAXV = 100.0
BIGM = 32768.0

NPT = 8
NSLOT = 6
STEP = 4

HOPS = (0.19, 0.2, 0.13, 0.08, 1.6)
P_PV, P_J, P_LN, P_EVAC, P_T2 = 0.1, -0.3, 0.4, -0.2, -0.1
LATE, EASY, SLOPE = 4.0, 0.2, 0.1
F_DUE, O_DUE, XT_DUE, QK_DUE, V_DUE = 5, 11, 2.4, 1.4, 0.7

ALU = mybir.AluOpType
ACT = mybir.ActivationFunctionType
F32 = mybir.dt.float32
F16 = mybir.dt.float16
I32 = mybir.dt.int32


class Queue:

    def __init__(self):
        self.items = []
        self.seen = {}

    def add(self, fn, waits=(), inc=None):
        need = {}
        for t in waits:
            if t is None:
                continue
            s, v = t
            if self.seen.get(id(s), 0) < v:
                need[id(s)] = (s, max(v, need.get(id(s), (s, 0))[1]))
        for k, (s, v) in need.items():
            self.seen[k] = v
        self.items.append((list(need.values()), fn, inc))

    def run(self, eng):
        for waits, fn, inc in self.items:
            for s, v in waits:
                eng.wait_ge(s, v)
            ins = fn(eng)
            if inc is not None:
                ins.then_inc(inc[0], inc[1])


class Count:

    def __init__(self, sem, step=1):
        self.sem, self.step, self.n = sem, step, 0

    def inc(self):
        self.n += self.step
        return (self.sem, self.step)

    @property
    def token(self):
        return (self.sem, self.n) if self.n else None


class Bank:

    def __init__(self):
        self.held, self.tokens = False, []

    def give(self, *tokens):
        self.held, self.tokens = False, list(tokens)


class Op:

    def __init__(self, queue, cost, fns, waits, count, prio=0.0, bank=None, each=False):
        self.queue, self.cost, self.fns = queue, cost, fns if isinstance(fns, list) else [fns]
        self.waits, self.count, self.prio, self.bank, self.each = waits, count, prio, bank, each


class Order:

    def __init__(self, hops):
        self.free, self.ready, self.strands = {}, {}, []
        self.hops = {id(q): hop for q, hop in hops}

    def add(self, gen):
        self.step(gen, None)

    def step(self, gen, token):
        try:
            self.strands.append((gen, gen.send(token)))
        except StopIteration:
            pass

    def run(self):
        while self.strands:
            best = None
            for k, (gen, op) in enumerate(self.strands):
                if op.bank is not None and op.bank.held:
                    continue
                try:
                    waits = op.waits() if callable(op.waits) else op.waits
                except KeyError:
                    continue
                if op.bank is not None:
                    waits = [*waits, *op.bank.tokens]
                start = self.free.get(id(op.queue), 0.0)
                for t in waits:
                    if t is not None:
                        start = max(start, self.ready[id(t[0]), t[1]])
                prio = op.prio() if callable(op.prio) else op.prio
                if best is None or start + prio < best[0]:
                    best = (start + prio, start, k, gen, op, waits)
            assert best is not None, "no strand can go on"
            _, start, k, gen, op, waits = best
            del self.strands[k]
            if op.bank is not None:
                op.bank.held = True
            for n, fn in enumerate(op.fns):
                last = n == len(op.fns) - 1
                op.queue.add(fn, waits if n == 0 else (), op.count.inc() if op.count and (last or op.each) else None)
            end = self.free[id(op.queue)] = start + op.cost
            token = None
            if op.count:
                token = op.count.token
                self.ready[id(token[0]), token[1]] = end + self.hops[id(op.queue)]
            self.step(gen, token)


def build(nc, x, wqT, wkT, wvT, woT, wfT, bqk_in, bv, bo, fsc, fbi, idf, idh, mq, mk, zrow, out):
    ctx = ExitStack()
    with ctx:
        def sb(name, shape, dt):
            return ctx.enter_context(nc.sbuf_tensor(name, shape, dt))

        def pb(name, shape, dt):
            return ctx.enter_context(nc.psum_tensor(name, shape, dt))

        def cnt(name, step=1):
            return Count(ctx.enter_context(nc.semaphore(name)), step)

        Wh = {k: sb(f"wh_{k}", [P, 4, D], F16) for k in "qkvo"}
        Wl = {k: sb(f"wl_{k}", [P, 4, D], F16) for k in "qkvo"}
        Wf = sb("wf", [P, 4, D], F16)
        xTh = [sb(f"xTh{i}", [P, 4, L], F16) for i in range(2)]
        xTl = [sb(f"xTl{i}", [P, 4, L], F16) for i in range(2)]
        Q4 = [sb(f"Q4_{i}", [P, 4, L], F16) for i in range(2)]
        K4 = [sb(f"K4_{i}", [P, 4, L], F16) for i in range(2)]
        sgh = [sb(f"sgh{i}", [P, L], F16) for i in range(2)]
        sgl = [sb(f"sgl{i}", [P, L], F16) for i in range(2)]
        V = sb("V", [P, NSLOT, NT, P], F32)
        PT = sb("PT", [P, NPT, 512], F32)
        Onh = sb("Onh", [P, NSLOT, L], F16)
        Onl = sb("Onl", [P, NSLOT, L], F16)
        xs = sb("xs", [P, NT, D], F32)
        xr = [sb(f"xr{i}", [P, D], F32) for i in range(2)]
        Y = sb("Y", [P, D], F32)
        E = sb("E", [P, D], F32)
        Z = sb("Z", [P, D], F32)
        U = sb("U", [P, D], F32)
        T1 = sb("T1", [P, D], F32)
        Sw = sb("Sw", [P, 4, P], F32)
        Rsb = sb("Rsb", [P, 512], F32)
        Tn = sb("Tn", [P, 512], F32)
        bvb = sb("bvb", [P, D], F32)
        bob = sb("bob", [P, D], F32)
        fsb = sb("fsb", [P, D], F32)
        fbb = sb("fbb", [P, D], F32)
        identf = sb("identf", [P, P], F32)
        identh = sb("identh", [P, P], F16)
        bqk0 = sb("bqk0", [P, 2, NG], F32)
        bqk = sb("bqk", [P, 2, NG], F32)
        st6 = sb("st6", [P, NT, 6], F32)
        mv = sb("mv", [P, NT, 2], F32)
        rs = sb("rs", [P, 3, NT], F32)
        junk = sb("junk", [P, 2, L], mybir.dt.bfloat16)
        a16 = sb("a16", [P, 2, 16], F16)
        sums = sb("sums", [P, 2, 16], F32)
        rsum = sb("rsum", [P, 2, 16], F32)
        cT = sb("cT", [16, 2, P], F16)

        pS = [pb(f"pS{i}", [P, 1024], F32) for i in range(2)]
        pT = [pb(f"pT{i}", [P, 512], F32) for i in range(2)]
        pO = pb("pO", [P, 512], F32)
        pJ = pb("pJ", [P, 512], F32)
        pJc = pJ[0:16, 0:64].bitcast(F16)

        pe, act, dve, pool, sp = Queue(), Queue(), Queue(), Queue(), Queue()
        c_const = cnt("s_const", 16)
        c_w = {k: cnt(f"s_w{k}", 16) for k in "qkvof"}
        c_wh = cnt("s_wh")
        c_wl = cnt("s_wl")
        c_b = cnt("s_b")
        c_x = [cnt(f"s_x{i}", 16) for i in range(NT)]
        c_r = [cnt(f"s_r{i}", 16) for i in range(2)]
        c_o = [cnt(f"s_o{i}", 16) for i in range(2)]
        c_ln = cnt("s_ln")
        c_pj = cnt("s_pj")
        c_xh = cnt("s_xh")
        c_xl = cnt("s_xl")
        c_qh = cnt("s_qh")
        c_ql = cnt("s_ql")
        c_qd = [cnt(f"s_qd{i}", 16) for i in range(2)]
        c_sd = [cnt(f"s_sd{i}", 16) for i in range(2)]
        c_id = cnt("s_id", 16)
        c_s0 = [cnt(f"s_s0{i}", 16) for i in range(2)]
        c_v = cnt("s_v")
        c_S = cnt("s_S")
        c_a = cnt("s_a")
        c_se = cnt("s_se")
        c_rs = cnt("s_rs")
        c_sw = cnt("s_sw")
        c_ct = cnt("s_ct")
        c_cd = [cnt(f"s_cd{i}", 16) for i in range(2)]
        c_T = cnt("s_T")
        c_p = cnt("s_p")
        c_pv = cnt("s_pv")
        c_R = cnt("s_R")
        c_dv = cnt("s_dv")
        c_oh = cnt("s_oh")
        c_ol = cnt("s_ol")
        c_g = cnt("s_g")
        c_gt = cnt("s_gt")
        c_y2 = cnt("s_y2")
        c_e = cnt("s_e")
        c_t1 = cnt("s_t1")
        c_t2 = cnt("s_t2")
        c_f = cnt("s_f")

        bank = Bank()
        order = Order(zip((pe, act, dve, pool, sp), HOPS))
        reached = [0.0]

        def need_by(unit):
            return lambda: min(EASY, max(0.0, SLOPE * (unit - reached[0] - LATE)))

        def copy_in(dst, src):
            return lambda e: e.dma_start(dst, src)

        def constants():
            const["id"] = yield Op(sp, 0.65, copy_in(identf[:, :], idf), [], c_id, -9.0)
            fns = [copy_in(identh[:, :], idh), copy_in(bqk0[:, :, :], bqk_in)]
            for t, v in ((bvb, bv), (bob, bo), (fsb, fsc), (fbb, fbi)):
                fns.append(copy_in(t[:, :], v.rearrange("(a d) -> a d", a=1).broadcast_to([P, D])))
            for i in range(2):
                for j in range(4):
                    fns += [copy_in(Q4[i][96:128, j, :], mq), copy_in(K4[i][96:128, j, :], mk)]
            const["in"] = yield Op(sp, 0.65 * len(fns), fns, [], c_const, -1.2, each=True)

        const = {}

        def small_constants():
            yield Op(dve, 0.1, lambda e: e.tensor_scalar(bqk[:, 0, :], bqk0[:, 0, :], SQ, None, ALU.mult),
                     lambda: [const["in"]], c_b)
            const["bias"] = yield Op(dve, 0.1, lambda e: e.tensor_scalar(bqk[:, 1, :], bqk0[:, 1, :], SW, None,
                                                                         ALU.mult), lambda: [const["in"]], c_b)

        wsrc = {"q": wqT, "k": wkT, "v": wvT, "f": wfT, "o": woT}
        w_tok, stage_free = {}, {}

        def load_weights():
            for i, (key, src) in enumerate(wsrc.items()):
                dst = PT[:, 4 * (i % 2):4 * (i % 2) + 4, :]
                w_tok["in", key] = yield Op(sp, 1.0, copy_in(dst, src),
                                            lambda: [stage_free[i - 2]] if i > 1 else [], c_w[key], -4.0)

        def split_weights():
            for i, key in enumerate(wsrc):
                src = PT[:, 4 * (i % 2):4 * (i % 2) + 4, :]
                loaded = lambda key=key: [w_tok["in", key]]
                if key == "f":
                    t = yield Op(dve, 1.1, lambda e, src=src: e.tensor_scalar(src, src, 0.0, 2.0, ALU.is_ge, ALU.mult),
                                 loaded, c_wl, -0.2)
                    w_tok[key] = stage_free[i] = yield Op(
                        dve, 1.1, lambda e, src=src: e.tensor_scalar(Wf[:, :, :], src, -1.0, None, ALU.add), [t], c_wl, -0.2)
                    continue
                sc = SQ if key == "q" else SW
                for h in range(4):
                    t = yield Op(act, 0.52, lambda e, src=src, key=key, sc=sc, h=h: e.activation(
                        Wh[key][:, h, :], src[:, h, :], ACT.Copy, scale=sc), loaded, c_wh, -0.2)
                    w_tok[key] = yield Op(dve, 0.6, lambda e, src=src, key=key, sc=sc, h=h: e.scalar_tensor_tensor(
                        Wl[key][:, h, :], src[:, h, :], sc, Wh[key][:, h, :], ALU.mult, ALU.subtract), [t], c_wl, -0.2)
                stage_free[i] = w_tok[key]
            for k in range(NPT):
                pvtok[k - NPT] = w_tok["o"]

        x_view = x.rearrange("b (w t r) d -> b t w r d", w=4, t=NT)
        x_rows = x.rearrange("b (w t r) d -> b w r t d", w=4, t=NT)
        o_view = out.rearrange("b (w t r) d -> b t w r d", w=4, t=NT)
        x_tok, xs_free, ln_tok, xt_tok, ff_tok, fo_tok = {}, {}, {}, {}, {}, {}

        def load_x():
            for b in range(B):
                for h in range(2) if b == 0 else (0,):
                    ts = slice(4 * h, 4 * h + 4) if b == 0 else slice(0, NT)
                    for w in range(4):
                        tok = yield Op(sp, 0.65, copy_in(xs[32 * w:32 * w + 32, ts, :], x_rows[b, w, :, ts, :]),
                                       lambda: [xs_free[b - 1, NT - 1]] if b else [], c_x[h],
                                       P_LN if b else (-1.0, -8.0)[h == 0])
                    for t in range(NT)[ts]:
                        loaded[b, t] = tok

        loaded = {}

        def layer_norm():
            last = None
            for b, ts in [(0, range(4)), (0, range(4, NT)), *((b, range(NT)) for b in range(1, B))]:
                v, y, z = (rs[:, k, ts[0]:ts[-1] + 1] for k in range(3))
                var = mv[:, ts[0]:ts[-1] + 1, 1]
                prio = -0.1 if b == 0 else P_LN
                for t in ts:
                    st = yield Op(dve, 0.6, lambda e, t=t: e.bn_stats(st6[:, t, :], xs[:, t, :]),
                                  lambda: [loaded[b, t], last], c_ln, prio)
                    last = yield Op(dve, 0.1, lambda e, t=t: e.bn_aggr(mv[:, t, :], st6[:, t, :]), [st], c_ln, prio)
                ops = [lambda e, v=v, var=var: e.tensor_scalar(v, var, EPS, None, ALU.add),
                       lambda e, v=v, z=z: e.tensor_scalar(z.bitcast(I32), v.bitcast(I32), 1, None,
                                                           ALU.logical_shift_right),
                       lambda e, y=y, z=z: e.tensor_scalar(y.bitcast(I32), z.bitcast(I32), -1.0, 1597463007.0,
                                                           ALU.mult, ALU.add)]
                for _ in range(3):
                    ops += [lambda e, y=y, z=z: e.tensor_tensor(z, y, y, ALU.mult),
                            lambda e, v=v, z=z: e.tensor_tensor(z, z, v, ALU.mult),
                            lambda e, z=z: e.tensor_scalar(z, z, -0.5, 1.5, ALU.mult, ALU.add),
                            lambda e, y=y, z=z: e.tensor_tensor(y, y, z, ALU.mult)]
                for f in ops:
                    last = yield Op(dve, 0.07, f, [last], c_ln, prio)
                for t in ts:
                    ln_tok[b, t] = yield Op(dve, 0.35, lambda e, t=t: e.tensor_scalar(
                        xs[:, t, :], xs[:, t, :], mv[:, t, 0:1], rs[:, 1, t:t + 1], ALU.subtract, ALU.mult),
                        [last], c_ln, prio)
                last = ln_tok[b, ts[-1]]

        def transpose_x(b):
            d = b % 2
            for t in range(NT):
                fns = [lambda e, t=t, c=c: e.transpose(pJ[:, c * P:(c + 1) * P], xs[:, t, c * P:(c + 1) * P],
                                                       identf[:, :]) for c in range(4)]
                tok = yield Op(pe, 0.44, fns, lambda: [ln_tok[b, t], const["id"], ff_tok[b - 2, t] if b > 1
                                                       else None], c_pj, need_by(8 * b - XT_DUE + 0.1 * t if b or t < 4 else LATE + 0.1 * t), bank)
                xs_free[b, t] = tok
                hi = xTh[d][:, :, t * P:(t + 1) * P]
                lo = xTl[d][:, :, t * P:(t + 1) * P]
                src = pJ[:, :].rearrange("p (c q) -> p c q", c=4)
                high = yield Op(dve, 0.6, lambda e, hi=hi: e.tensor_copy(hi, src), [tok], c_xh, P_EVAC)
                low = yield Op(dve, 0.6, lambda e, hi=hi, lo=lo: e.tensor_tensor(lo, src, hi, ALU.subtract),
                               [high], c_xl, P_EVAC)
                bank.give(high, low)
                xt_tok[b, t] = (high, low)

        def product(terms, waits, prio):
            tok = None
            for k in range(0, len(terms), STEP):
                fns = [lambda e, a=a, b_=b_, n=k + n: e.matmul(pJ[:, :], a, b_, start=n == 0,
                                                               stop=n == len(terms) - 1)
                       for n, (a, b_) in enumerate(terms[k:k + STEP])]
                last = k + STEP >= len(terms)
                tok = yield Op(pe, 0.216 * len(fns), fns, waits if k == 0 else [], c_pj if last else None, prio,
                               bank if k == 0 else None)
            return tok

        staged, qk_tok, grp_S, grp_T = {}, {}, {}, {}

        def project_qk():
            for gn in range(B * NG):
                b, g = divmod(gn, NG)
                d = b % 2
                for which, half in ((0, 0), (1, 0), (0, 1), (1, 1)):
                    key = "qk"[which]
                    cs = slice(half * 512, half * 512 + 512)
                    terms = []
                    for c in range(4):
                        wh, wl = Wh[key][:, c, g * P:(g + 1) * P], Wl[key][:, c, g * P:(g + 1) * P]
                        terms += [(wh, xTh[d][:, c, cs]), (wl, xTh[d][:, c, cs]), (wh, xTl[d][:, c, cs])]

                    def waits(key=key, which=which, half=half, gn=gn, b=b):
                        placed = [qk_tok[gn - 1, which, half]] if gn else []
                        return [w_tok[key], const["bias"], *xt_tok[b, 4 * half + 3], *placed]
                    tok = yield from product(terms, waits, need_by(2 * gn - QK_DUE + 0.1 * (2 * half + which)))
                    order.add(stage_qk(gn, which, half, tok))

        def stage_qk(gn, which, half, tok):
            cs = slice(half * 512, half * 512 + 512)
            bias = bqk[:, which, gn % NG:gn % NG + 1]
            hi, lo = sgh[which][:, cs], sgl[which][:, cs]
            placed = qk_tok[gn - 1, which, half] if gn else None
            high = yield Op(act, 0.57, lambda e: e.activation(hi, pJ[:, :], ACT.Identity, bias=bias),
                            [tok, const["bias"], placed], c_qh, P_EVAC)
            low = yield Op(dve, 0.66, lambda e: e.scalar_tensor_tensor(lo, pJ[:, :], bias, hi, ALU.add, ALU.subtract),
                           [high, placed], c_ql, P_EVAC)
            bank.give(high, low)
            staged[gn, which, half] = (high, low)

        def place_qk():
            for gn in range(B * NG):
                for which, half in ((0, 0), (1, 0), (0, 1), (1, 1)) if gn == 0 else ((0, None), (1, None)):
                    count = c_s0[which] if half == 0 else c_sd[which]
                    dst = (Q4, K4)[which][gn % 2]
                    halves = (half,) if half is not None else (0, 1)
                    cs = slice(512 * halves[0], 512 * halves[-1] + 512)

                    def waits(gn=gn, which=which, halves=halves):
                        free = [grp_S[gn - 2], grp_T[gn - 2]] if gn > 1 else []
                        return [t for h in halves for t in staged[gn, which, h]] + [const["in"]] + free
                    parts = (sgh, sgl, sgh) if which == 0 else (sgh, sgh, sgl)
                    for r, s in enumerate(parts):
                        for j in range(4):
                            tok = yield Op(sp, 0.65, copy_in(dst[32 * r:32 * r + 32, j, cs],
                                                             s[which][32 * j:32 * j + 32, cs]), waits, count, 0.1)
                    if which == 0:
                        tok = yield Op(sp, 0.65, copy_in(dst[96:97, :, cs], zrow[:, :, cs]), waits, count, 0.1)
                    for h in halves:
                        qk_tok[gn, which, h] = tok

        v_tok, pv_last = {}, {}

        def project_v(b):
            d = b % 2
            for t in range(NT):
                ts = slice(t * P, (t + 1) * P)
                terms = []
                for c in range(4):
                    terms += [(xTh[d][:, c, ts], Wh["v"][:, c, :]), (xTh[d][:, c, ts], Wl["v"][:, c, :]),
                              (xTl[d][:, c, ts], Wh["v"][:, c, :])]

                def waits(t=t):
                    for g in range(NG):
                        if NG * b + g >= NSLOT:
                            pv_last[NG * b + g - NSLOT]
                    return [w_tok["v"], *xt_tok[b, t]]
                tok = yield from product(terms, waits, need_by(8 * b - V_DUE + 0.3 * t / 8 if b else LATE + 0.5 + 0.1 * t))
                order.add(store_v(b, t, tok))

        def store_v(b, t, tok):
            g = 0
            while g < NG:
                s = (NG * b + g) % NSLOT
                n = min(NG - g, NSLOT - s)
                cols = slice(g * P, (g + n) * P)
                dst = V[:, s:s + n, t, :]
                free = [pv_last[NG * b + k - NSLOT] for k in range(g, g + n) if NG * b + k >= NSLOT]
                tok_v = yield Op(dve, 0.07 + 0.133 * n, lambda e, cols=cols, dst=dst, n=n: e.scalar_tensor_tensor(
                    dst, pJ[:, cols].rearrange("p (n q) -> p n q", n=n), 1.0 / SW,
                    bvb[:, cols].rearrange("p (n q) -> p n q", n=n), ALU.mult, ALU.add),
                    [tok, const["in"], *free], c_v, P_EVAC)
                g += n
            bank.give(tok_v)
            v_tok[b, t] = tok_v

        gate_tok, t2_tok, f_tok = {}, {}, {}

        def gates(b):
            yield from gate_or_output(b, 0)

        def results(b):
            yield from gate_or_output(b, 1)

        def gate_or_output(b, part):
            d = b % 2
            for t in range(NT):
                i = b * NT + t
                ts = slice(t * P, (t + 1) * P)
                ft, ot = [], []
                for c in range(4):
                    ft += [(xTh[d][:, c, ts], Wf[:, c, :]), (xTl[d][:, c, ts], Wf[:, c, :])]
                for g in range(NG):
                    n = (NG * b + g) % NSLOT
                    ot += [(Onh[:, n, ts], Wh["o"][:, g, :]), (Onh[:, n, ts], Wl["o"][:, g, :]),
                           (Onl[:, n, ts], Wh["o"][:, g, :])]
                unit = 8 * b + 6 + t // 4
                if part == 0:
                    tok = yield from product(ft, lambda: [w_tok["f"], *xt_tok[b, t], gate_tok[i - 1] if i else None],
                                             need_by(8 * b + (F_DUE if b < B - 1 else 2) + 0.1 * t))
                    ff_tok[b, t] = tok
                    order.add(gate(i, b, t, tok))
                else:
                    unit = 8 * b + 6 + t // 4

                    def waits():
                        if i:
                            f_tok[i - 1]
                        return [w_tok["o"], oh_tok[unit], ol_tok[unit]]
                    tok = yield from product(ot, waits,
                                             need_by(8 * b + O_DUE))
                    fo_tok[b, t] = tok
                    order.add(result(i, b, t, tok))

        def gate(i, b, t, tok):
            s = i % 2
            last = gate_tok[i - 1] if i else None
            G = xs[:, t, :] if b == B - 1 else U[:, :]
            y1 = yield Op(dve, 0.6, lambda e: e.tensor_tensor(Y[:, :], pJ[:, :], fsb[:, :], ALU.mult),
                          [tok, const["in"], last], c_g, P_EVAC)
            bank.give(y1)
            y2 = yield Op(pool, 1.11, lambda e: e.tensor_tensor(Y[:, :], Y[:, :], fbb[:, :], ALU.add), [y1], c_y2)
            e1 = yield Op(dve, 0.34, lambda e: e.tensor_scalar(E[:, :], Y[:, :], MAXV, -87.0, ALU.min, ALU.max),
                          [y2], c_g)
            y3 = yield Op(dve, 0.34, lambda e: e.tensor_scalar(Y[:, :], Y[:, :], MAXV, -MAXV, ALU.min, ALU.max),
                          [y2], c_g)
            e2 = yield Op(act, 0.52, lambda e: e.activation(E[:, :], E[:, :], ACT.Exp, scale=-1.0), [e1], c_e)
            e3 = yield Op(dve, 0.34, lambda e: e.tensor_scalar(E[:, :], E[:, :], 1.0, None, ALU.add), [e2], c_g)
            z = yield Op(dve, 0.34, lambda e: e.tensor_scalar(Z[:, :].bitcast(I32), E[:, :].bitcast(I32), -1.0,
                                                              2129859011.0, ALU.mult, ALU.add), [e3], c_g)

            def u_free():
                return [t2_tok[min(i - 1, (B - 1) * NT - 1)]] if i else []
            for k in range(3):
                u = yield Op(pool, 1.22, lambda e: e.tensor_tensor(U[:, :], E[:, :], Z[:, :], ALU.mult),
                             lambda: [z, *u_free()], c_gt)
                z = yield Op(dve, 0.6, lambda e, k=k: e.scalar_tensor_tensor(
                    Z[:, :], U[:, :], 2.0 if k else -2.0, Z[:, :], ALU.add, ALU.mult), [u], c_g)
            gate_tok[i] = yield Op(pool, 1.22, lambda e: e.tensor_tensor(G, Y[:, :], Z[:, :], ALU.mult),
                                   [z, y3, xs_free[b, t]], c_gt)

        def reload_x(i, b, t):
            s = i % 2
            xr_full[i] = yield Op(sp, 0.65, copy_in(xr[s][:, :], x_view[b, t]),
                                  lambda: [stored[i - 2]] if i > 1 else [], c_r[s], 0.2)

        xr_full, stored = {}, {}

        def result(i, b, t, tok):
            s = i % 2
            order.add(reload_x(i, b, t))
            G = xs[:, t, :] if b == B - 1 else U[:, :]
            t1 = yield Op(dve, 0.6, lambda e: e.scalar_tensor_tensor(T1[:, :], pJ[:, :], -SS, bob[:, :], ALU.mult,
                                                                     ALU.subtract),
                          [tok, const["in"], f_tok[i - 1] if i else None], c_t1, P_EVAC)
            bank.give(t1)
            t2 = t2_tok[i] = yield Op(pool, 1.22, lambda e: e.tensor_tensor(T1[:, :], T1[:, :], G, ALU.mult),
                                      lambda: [t1, gate_tok[i]], c_t2, P_T2)
            f = f_tok[i] = yield Op(pool, 1.22, lambda e: e.tensor_tensor(xr[s][:, :], T1[:, :], xr[s][:, :], ALU.add),
                                    lambda: [t2, xr_full[i]], c_f)
            stored[i] = yield Op(sp, 0.65, copy_in(o_view[b, t], xr[s][:, :]), [f], c_o[s], 0.2)

        NU = B * NG * NQS
        s_tiles = [(m, qi, j) for m in range(NU) for qi in range(4) for j in range(4)]
        slots, before, used, at = [], [], {}, 0
        for i, (m, qi, j) in enumerate(s_tiles):
            wide = 4 * (m % NQS) + qi + 1 > 4
            at = (at + at % 2) % 4 if wide else at
            banks = (at, at + 1) if wide else (at,)
            slots.append(pS[at // 2][:, 512 * (at % 2):512 * (at % 2) + (1024 if wide else 512)])
            before.append(sorted({used[k] for k in banks if k in used}))
            used.update({k: i for k in banks})
            at = (at + len(banks)) % 4
        S_tok, se_tok, a_tok, a_last, se_last = {}, {}, {}, {}, {}
        a16_free, sums_free, cdma = {}, {}, {}

        def scores():
            for i, (m, qi, j) in enumerate(s_tiles):
                gn, qs = divmod(m, NQS)
                u, qb, slot = gn % 2, 4 * qs + qi, slots[i]
                qc = slice(qb * P, qb * P + P)
                fns, cost = [], 0.056
                for k0 in range(0, qb * P, 512):
                    k1 = min(k0 + 512, qb * P)
                    cost += (k1 - k0) * 0.216 / 512
                    fns.append(lambda e, k0=k0, k1=k1, slot=slot, u=u, j=j, qc=qc: e.matmul(
                        slot[:, k0:k1], Q4[u][0:96, j, qc], K4[u][0:96, j, k0:k1], start=True, stop=True))
                fns.append(lambda e, slot=slot, u=u, j=j, qc=qc: e.matmul(
                    slot[:, qc], Q4[u][:, j, qc], K4[u][:, j, qc], start=True, stop=True))

                def waits():
                    placed = [qk_tok[gn, w, h] for w in range(2) for h in range(qs + 1)]
                    return [*(se_tok[p] for p in before[i]), *placed]
                S_tok[i] = yield Op(pe, cost, fns, waits, c_S)
                grp_S[gn] = S_tok[i] if (qs, qi, j) == (1, 3, 3) else None
                if grp_S[gn] is None:
                    del grp_S[gn]

        def shifts():
            for i, (m, qi, j) in enumerate(s_tiles):
                par, col, width = m % 2, 4 * j + qi, (4 * (m % NQS) + qi + 1) * P
                a_tok[i] = yield Op(dve, 0.065 + 0.00104 * width, lambda e, i=i, width=width, par=par, col=col:
                                    e.tensor_scalar(junk[:, i % 2, 0:width], slots[i][:, 0:width], -SS, 3e38,
                                                    ALU.mult, ALU.min, accum_out=a16[:, par, col:col + 1]),
                                    lambda: [S_tok[i], a16_free[m - 2] if m > 1 else None, a_tok.get(i - 2)], c_a)
                if (qi, j) == (3, 3):
                    a_last[m] = a_tok[i]

        def row_sums():
            for i, (m, qi, j) in enumerate(s_tiles):
                par, col, width = m % 2, 4 * j + qi, (4 * (m % NQS) + qi + 1) * P
                se_tok[i] = yield Op(act, 0.24 + 0.000833 * width, lambda e, i=i, width=width, par=par, col=col:
                                     e.activation(slots[i][:, 0:width], slots[i][:, 0:width], ACT.Exp,
                                                  bias=a16[:, par, col:col + 1], scale=SS,
                                                  accum_out=sums[:, par, col:col + 1]),
                                     lambda: [a_tok[i], sums_free[m - 2] if m > 1 else None], c_se)
                if (qi, j) == (3, 3):
                    se_last[m] = se_tok[i]

        def shift_rows():
            for m in range(NU):
                gn, qs = divmod(m, NQS)
                u, par = gn % 2, m % 2
                tok = yield Op(pe, 0.06, lambda e, par=par: e.transpose(pJc, a16[:, par, :], identh[:, :]),
                               lambda: [a_last[m], const["in"], cdma[m - 2] if m > 1 else None], c_pj, P_J, bank)
                a16_free[m] = tok
                ct = yield Op(dve, 0.13, lambda e, par=par: e.tensor_copy(cT[:, par, :], pJc),
                              [tok, cdma.get(m - 2)], c_ct, P_EVAC)
                bank.give(ct)
                fns = [copy_in(Q4[u][96:97, j, qs * 512:qs * 512 + 512], cT[4 * j:4 * j + 4, par, :])
                       for j in range(4)]
                cdma[m] = yield Op(sp, 2.6, fns, [ct], c_cd[par], -2.0, each=True)

        t_tiles = []
        for n in range(NU):
            for kb in range(4 * (n % NQS) + 4):
                width = 512 - max(0, P * (kb - 4 * (n % NQS)))
                heads = max(h for h in (1, 2, 4) if h * width <= 512)
                t_tiles += [(n, kb, width, range(j, j + heads)) for j in range(0, 4, heads)]
        T_tok, p_tok, pvtok, pv_tok, o_free = {}, {}, {}, {}, {}

        def scores_t():
            for i, (n, kb, width, heads) in enumerate(t_tiles):
                gn, qs = divmod(n, NQS)
                u, slot = gn % 2, pT[i % 2]
                kc = slice(kb * P, kb * P + P)
                end = 512 * qs + 512
                fns, cost = [], 0.0
                for k, j in enumerate(heads):
                    at, q0 = k * width, end - width
                    if kb >= 4 * qs:
                        cost += 0.056
                        fns.append(lambda e, slot=slot, u=u, j=j, kc=kc, at=at, q0=q0: e.matmul(
                            slot[:, at:at + P], K4[u][:, j, kc], Q4[u][:, j, q0:q0 + P], start=True, stop=True))
                        at, q0 = at + P, q0 + P
                    if q0 < end:
                        cost += (end - q0) * 0.216 / 512
                        fns.append(lambda e, slot=slot, u=u, j=j, kc=kc, at=at, q0=q0, end=end: e.matmul(
                            slot[:, at:at + end - q0], K4[u][0:97, j, kc], Q4[u][0:97, j, q0:end],
                            start=True, stop=True))
                T_tok[i] = yield Op(pe, cost, fns, lambda: [p_tok[i - 2] if i > 1 else None, cdma[n]], c_T)
                if (qs, kb) == (1, 7):
                    grp_T[gn] = T_tok[i]

        def probabilities():
            for i, (n, kb, width, heads) in enumerate(t_tiles):
                cols = width * len(heads)
                p_tok[i] = yield Op(act, 0.052 + 0.000833 * cols, lambda e, i=i, cols=cols: e.activation(
                    PT[:, i % NPT, 0:cols], pT[i % 2][:, 0:cols], ACT.Exp, scale=SS),
                    lambda: [T_tok[i], pvtok[i - NPT]], c_p)

        def outputs():
            for i, (n, kb, width, heads) in enumerate(t_tiles):
                gn, qs = divmod(n, NQS)
                s, b, nkb = gn % NSLOT, gn // NG, 4 * qs + 4
                for k, j in enumerate(heads):
                    fn = (lambda e, k=k, j=j, i=i, s=s, kb=kb, width=width, last=kb == nkb - 1: e.matmul(
                        pO[32 * j:32 * j + 32, 512 - width:512], V[:, s, kb, 32 * j:32 * j + 32],
                        PT[:, i % NPT, k * width:k * width + width], start=kb == 0, stop=last))
                    tok = yield Op(pe, width * 0.234 / 512, fn, lambda: [p_tok[i], v_tok[b, kb], o_free[n - 1]
                                                                        if n and kb == 0 else None], c_pv, P_PV)
                pvtok[i] = tok
                reached[0] = n + (kb + 1) / nkb
                if i + 1 == len(t_tiles) or t_tiles[i + 1][0] != n:
                    pv_tok[n] = tok
                    if qs == 1:
                        pv_last[gn] = tok

        rs_free, sw_free, R_tok, dv_tok, oh_tok, ol_tok = {}, {}, {}, {}, {}, {}

        def inverse_sums():
            for n in range(NU):
                par = n % 2
                sv = rsum[:, par, :].rearrange("p (j q o) -> p q j o", j=4, o=1)
                r = yield Op(dve, 0.17, lambda e, par=par: e.reciprocal(rsum[:, par, :], sums[:, par, :]),
                             lambda: [se_last[n], rs_free.get(n - 2)], c_rs, 0.2)
                sw = yield Op(dve, 0.35, lambda e, sv=sv: e.tensor_copy(
                    Sw[:, :, :].rearrange("p q (j r) -> p q j r", j=4), sv.broadcast_to([P, 4, 4, 32])),
                    lambda: [r, sw_free.get(n - 1)], c_sw, 0.2)
                sums_free[n], rs_free[n] = r, sw
                fns = [lambda e, qi=qi: e.transpose(pJ[:, qi * P:(qi + 1) * P], Sw[:, qi, :], identf[:, :])
                       for qi in range(4)]
                tok = yield Op(pe, 0.44, fns, lambda: [sw, const["id"], dv_tok[n - 1] if n else None], c_pj,
                               P_J, bank)
                sw_free[n] = tok
                R_tok[n] = yield Op(dve, 0.6, lambda e: e.tensor_scalar(Rsb[:, :], pJ[:, :], SW, None, ALU.mult),
                                    [tok, dv_tok.get(n - 1)], c_R, P_EVAC)
                bank.give(R_tok[n])

        def normalise():
            for n in range(NU):
                gn, qs = divmod(n, NQS)
                s = gn % NSLOT
                cs = slice(qs * 512, qs * 512 + 512)
                dv = yield Op(dve, 0.6, lambda e: e.tensor_tensor(Tn[:, :], pO[:, :], Rsb[:, :], ALU.mult),
                              lambda: [pv_tok[n], R_tok[n], ol_tok.get(n - 1)], c_dv, -0.3)
                o_free[n] = dv_tok[n] = dv
                oh_tok[n] = yield Op(dve, 0.34, lambda e, s=s, cs=cs: e.tensor_copy(Onh[:, s, cs], Tn[:, :]),
                                     lambda: [dv, fo_tok[(gn - NSLOT) // NG, 4 * qs + 3] if gn >= NSLOT else None],
                                     c_oh, 0.1)
                ol_tok[n] = yield Op(pool, 1.11, lambda e, s=s, cs=cs: e.tensor_tensor(
                    Onl[:, s, cs], Tn[:, :], Onh[:, s, cs], ALU.subtract), [oh_tok[n]], c_ol, -0.3)

        def chained(make):
            for b in range(B):
                yield from make(b)

        for strand in (load_x(), load_weights(), constants(), small_constants(), layer_norm(), split_weights(),
                       chained(transpose_x), project_qk(), place_qk(), chained(project_v), chained(gates), chained(results),
                       scores(), shifts(), row_sums(), shift_rows(), scores_t(), probabilities(), outputs(),
                       inverse_sums(), normalise()):
            order.add(strand)
        order.run()

        block = ctx.enter_context(nc.Block())

        @block.tensor
        def _(e):
            pe.run(e)

        @block.scalar
        def _(e):
            act.run(e)

        @block.vector
        def _(e):
            dve.run(e)

        @block.gpsimd
        def _(e):
            pool.run(e)

        @block.sync
        def _(e):
            sp.run(e)
            for c in c_o:
                e.wait_ge(*c.token)


def kernel(L0_attn_x, L0_attn_Wq, L0_attn_bq, L0_attn_Wk, L0_attn_bk, L0_attn_Wv, L0_attn_bv, L0_attn_Wo,
           L0_attn_bo, L0_ffn_weights, L0_ffn_scale, L0_ffn_bias):
    import concourse.bacc as bacc
    from concourse.bass_utils import run_bass_kernel_spmd

    def wt(w):
        return np.ascontiguousarray(np.asarray(w).T.reshape(4, P, D).transpose(1, 0, 2))

    r = np.arange(L) % 32
    c = np.arange(31)
    mq = np.zeros((32, L), np.float16)
    mk = np.zeros((32, L), np.float16)
    mq[1:] = np.where(c[:, None] == r[None, :], BIGM, 0.0)
    mk[1:] = np.where(c[:, None] < r[None, :], -BIGM, 0.0)
    mk[0] = SW * SW
    named = {
        "x": np.ascontiguousarray(L0_attn_x),
        "wqT": wt(L0_attn_Wq), "wkT": wt(L0_attn_Wk), "wvT": wt(L0_attn_Wv), "woT": wt(L0_attn_Wo),
        "wfT": wt(L0_ffn_weights),
        "bqk": np.ascontiguousarray(np.stack([np.asarray(v).reshape(NG, P).T for v in (L0_attn_bq, L0_attn_bk)], 1)),
        "bv": np.ascontiguousarray(L0_attn_bv), "bo": np.ascontiguousarray(L0_attn_bo),
        "fsc": np.ascontiguousarray(L0_ffn_scale), "fbi": np.ascontiguousarray(L0_ffn_bias),
        "idf": np.eye(P, dtype=np.float32), "idh": np.eye(P, dtype=np.float16),
        "mq": mq, "mk": mk, "zrow": np.zeros((1, 4, L), np.float16),
    }
    nc = bacc.Bacc("TRN2", target_bir_lowering=False, num_devices=1, dynamic_dma_scratch_size=1024)
    arrays, args = {}, []
    for name, a in named.items():
        arrays[f"in_{name}"] = a
        args.append(nc.dram_tensor(f"in_{name}", a.shape, mybir.dt.from_np(a.dtype), kind="ExternalInput").ap())
    out = nc.dram_tensor("out_0", (B, L, D), F32, kind="ExternalOutput").ap()
    build(nc, *args, out)
    res = run_bass_kernel_spmd(nc, [arrays], core_ids=[0])
    return res.results[0]["out_0"]
```
